# Optimizing a Trainium2 kernel written in Bass

```python
import numpy as np
import jax
import jax.numpy as jnp

def _softmax(x, axis=-1):
    return jax.nn.softmax(x, axis=axis)

def _gelu(x):
    return jax.nn.gelu(x, approximate=True)

def _silu(x):
    return jax.nn.silu(x)

def _sigmoid(x):
    return jax.nn.sigmoid(x)

def _layernorm(x, axis=-1, eps=1e-05):
    m = jnp.mean(x, axis=axis, keepdims=True)
    v = jnp.var(x, axis=axis, keepdims=True)
    return (x - m) / jnp.sqrt(v + eps)

def _scatter_add(tgt, idx, src, axis=0):
    return tgt.at[idx].add(src)

def _segment_sum(src, seg, n):
    return jax.ops.segment_sum(src, seg, n)
kernel_name = 'mk_macaron_d1_jaxref_r4_767e16'

def setup_inputs(seed: int=0):
    np.random.seed(seed)
    _w = jnp.asarray

    def _L0_attn_setup():
        import jax, jax.numpy as jnp
        import numpy as np
        EMBED = 256
        HEADS = 16
        key = jax.random.key(seed)
        ks = jax.random.split(key, 6)
        N, S = (1, 1024)
        half = EMBED // 2
        x = jax.random.normal(ks[0], (N, S, EMBED), dtype=jnp.float32)
        Wq = jax.random.normal(ks[1], (half, half), dtype=jnp.float32) * 0.02
        Wk = jax.random.normal(ks[2], (half, half), dtype=jnp.float32) * 0.02
        Wv = jax.random.normal(ks[3], (half, half), dtype=jnp.float32) * 0.02
        Wo = jax.random.normal(ks[4], (EMBED, half), dtype=jnp.float32) * 0.02
        bo = jnp.zeros((EMBED,), dtype=jnp.float32)
        return {'x': x, 'Wq': Wq, 'Wk': Wk, 'Wv': Wv, 'Wo': Wo, 'bo': bo}
    _L0_attn_in = _L0_attn_setup()

    def _L0_ffn_setup():
        import jax, jax.numpy as jnp
        import numpy as np
        B, N, D = (4, 512, 256)
        SPARSITY = 0.01
        key = jax.random.key(seed)
        k1, k2, k3 = jax.random.split(key, 3)
        x = jax.random.normal(k1, (B, N, D), dtype=jnp.float32)
        spatial = jax.random.normal(k2, (D, D), dtype=jnp.float32) * 0.02
        freq = jnp.fft.fft(spatial, axis=-1)
        k = int(D * SPARSITY)
        mag = jnp.abs(freq)
        kth = jax.lax.top_k(mag, k)[0][:, -1:]
        w_sparse = jnp.where(mag >= kth, freq, 0.0 + 0j)
        bias = jax.random.normal(k3, (D,), dtype=jnp.float32) * 0.01
        return {'x': x, 'w_freq_real': jnp.real(w_sparse).astype(jnp.float32), 'w_freq_imag': jnp.imag(w_sparse).astype(jnp.float32), 'bias': bias}
    _L0_ffn_in = _L0_ffn_setup()
    _d = {'L0_attn_x': _L0_attn_in['x'], 'L0_attn_Wq': _L0_attn_in['Wq'], 'L0_attn_Wk': _L0_attn_in['Wk'], 'L0_attn_Wv': _L0_attn_in['Wv'], 'L0_attn_Wo': _L0_attn_in['Wo'], 'L0_attn_bo': _L0_attn_in['bo'], 'L0_ffn_w_freq_real': _L0_ffn_in['w_freq_real'], 'L0_ffn_w_freq_imag': _L0_ffn_in['w_freq_imag'], 'L0_ffn_bias': _L0_ffn_in['bias']}
    _x0 = _d['L0_attn_x']
    _d['L0_attn_x'] = jax.random.normal(jax.random.fold_in(jax.random.key(seed), 1), (8, 512, 256), dtype=_x0.dtype)
    del _x0
    return _d

def reference(L0_attn_x, L0_attn_Wq, L0_attn_Wk, L0_attn_Wv, L0_attn_Wo, L0_attn_bo, L0_ffn_w_freq_real, L0_ffn_w_freq_imag, L0_ffn_bias):

    def _L0_attn_ref(x, Wq, Wk, Wv, Wo, bo):
        import jax, jax.numpy as jnp
        import numpy as np
        EMBED = 256
        HEADS = 16
        N, S, E = x.shape
        H = HEADS
        Dh = E // 2 // H
        scale = float(E // H) ** 0.5
        left = x[..., :E // 2]
        q = (left @ Wq.T).reshape(N, S, H, Dh)
        k = (left @ Wk.T).reshape(N, S, H, Dh)
        v = (left @ Wv.T).reshape(N, S, H, Dh)
        energy = jnp.einsum('nqhd,nkhd->nqkh', q, k)
        att = jax.nn.softmax(energy / scale, axis=2)
        out = jnp.einsum('nqkh,nkhd->nqhd', att, v)
        out = out.reshape(N, S, E // 2)
        return out @ Wo.T + bo

    def _L0_ffn_ref(x, w_freq_real, w_freq_imag, bias):
        import jax, jax.numpy as jnp
        import numpy as np
        B, N, D = (4, 512, 256)
        SPARSITY = 0.01
        w = jax.lax.complex(w_freq_real, w_freq_imag)
        x_freq = jnp.fft.fft(x, axis=-1)
        y_freq = jnp.einsum('bnd,do->bno', x_freq, w)
        y = jnp.real(jnp.fft.ifft(y_freq, axis=-1))
        return y + bias
    x = L0_attn_x
    x = x + 0.5 * _L0_ffn_ref(_layernorm(x, axis=-1), L0_ffn_w_freq_real, L0_ffn_w_freq_imag, L0_ffn_bias)
    x = x + _L0_attn_ref(_layernorm(x, axis=-1), L0_attn_Wq, L0_attn_Wk, L0_attn_Wv, L0_attn_Wo, L0_attn_bo)
    x = x + 0.5 * _L0_ffn_ref(_layernorm(x, axis=-1), L0_ffn_w_freq_real, L0_ffn_w_freq_imag, L0_ffn_bias)
    return x

_drawn_inputs = setup_inputs


def setup_inputs(seed=0):
    import zlib

    import numpy as np

    out = dict(_drawn_inputs(seed))
    spreads = {'L0_attn_bo': (0.0, 0.1)}
    factors = {'L0_attn_Wq': 8.0,
     'L0_attn_Wk': 8.0,
     'L0_attn_Wv': 8.0,
     'L0_attn_Wo': 8.0,
     'L0_ffn_bias': 6.884}
    for name, (base, spread) in spreads.items():
        noise = np.random.default_rng([zlib.crc32(name.encode()), seed]).standard_normal(out[name].shape)
        drawn = base * np.exp(spread * noise) if base else spread * noise
        out[name] = jnp.asarray(drawn.astype(out[name].dtype))
    for name, factor in factors.items():
        out[name] = (out[name] * factor).astype(out[name].dtype)
    return out
```

```python
import concourse.bass as bass
from concourse import mybir
from contextlib import ExitStack

F32 = mybir.dt.float32
BF16 = mybir.dt.bfloat16
I32 = mybir.dt.int32
ALU = mybir.AluOpType
ACT = mybir.ActivationFunctionType
AX = mybir.AxisListType

B, S, E = 8, 512, 256
H, Dh = 16, 8
HD = H * Dh
P = 128
T = S // P
C = E // P
PARTS = 3
TERMS = PARTS * PARTS
SROW = TERMS * Dh
ROWS = SROW + PARTS
EPS = 1e-5
SCORE_SCALE = 1.0 / float(E // H) ** 0.5
SAFE_SCORE = 60.0
SAFE_PRODUCT = (SAFE_SCORE / SCORE_SCALE) ** 2 / 1.05
NORM_POWER = -0.5

QUADS = 16
PAIRS = 2 * QUADS
PRING = 4
COL = 32
DEN = 16

PREFIX = {0: ["T1a", "T1b"], 2: ["F1a", "F1b"], 5: ["LT"], 6: ["QT", "KT"], 7: ["V"], 9: ["N"], 10: ["NT"]}
SUFFIX = {1: ["WOa", "WOb"], 4: ["T3a", "T3b"], 7: ["F2a"], 8: ["F2b"]}
GUARD_SLOT = 12
NPRE = sum(len(v) for v in PREFIX.values())
NSUF = sum(len(v) for v in SUFFIX.values())


PRE_NAMES = [n for v in PREFIX.values() for n in v]
PROLOGUE, EPILOGUE = -1, B


def static(v):
    return isinstance(v, int)


def ring_base(it):
    if static(it) and it <= 0:
        return 0 if it == PROLOGUE else NPRE
    if static(it) and it == EPILOGUE:
        return ring_base(B - 1) + NSUF
    return it * (NPRE + NSUF) + (NPRE - NSUF)


def jobs_of(it):
    pre = not (static(it) and it >= B - 1)
    suf = not (static(it) and it <= 0)
    return [(s, name) for s in range(QUADS)
            for name in (SUFFIX.get(s, []) if suf else []) + (PREFIX.get(s, []) if pre else [])]


def evac_count(name, it):
    return ring_base(it) + [n for _, n in jobs_of(it)].index(name) + 1


def quad_units(s):
    g, par, kt = s // 8, (s % 8) // 4, s % 4
    return g, par, kt, [8 * g + 2 * j + par for j in range(4)]


def build_macaron(nc, x, wq_t, wk_t, wv_t, wo_rows, w_re, w_im, bias, cos_tab, sin_tab, ident_in,
                  head_ones_in, out):
    x_v = x.rearrange("b (p t) e -> b p (t e)", t=T)
    out_v = out.rearrange("b (p t) e -> b p (t e)", t=T)

    q_scr = nc.dram_tensor("q_scr", [H, PARTS * Dh, S], BF16, kind="Internal").ap()
    k_scr = nc.dram_tensor("k_scr", [H, TERMS * Dh, S], BF16, kind="Internal").ap()

    ctx = ExitStack()
    with ctx:
        def sb(name, shape, dt=F32):
            return ctx.enter_context(nc.sbuf_tensor(name, shape, dt))

        def sem(name):
            return ctx.enter_context(nc.semaphore(name))

        ident = sb("ident", [P, P])
        head_ones = sb("head_ones", [P, 32], BF16)
        cos_sb = sb("cos_sb", [P, C, E])
        sin_sb = sb("sin_sb", [P, C, E])
        nsin_sb = sb("nsin_sb", [P, C, E])
        wre_sb = sb("wre_sb", [P, C, E])
        wim_sb = sb("wim_sb", [P, C, E])
        are_t = sb("are_t", [P, C, E])
        aim_t = sb("aim_t", [P, C, E])
        half_ffn = sb("half_ffn", [P, C, E])
        wq_sb = sb("wq_sb", [P, HD])
        wk_sb = sb("wk_sb", [P, HD])
        wv_sb = sb("wv_sb", [P, HD])
        wo_sb = sb("wo_sb", [P, 2, E])
        bias_raw = sb("bias_raw", [P, E])
        half_bias = sb("half_bias", [P, E])
        power = sb("power", [P, T])
        x_in = [sb(f"x_in{i}", [P, T, E]) for i in range(2)]
        x1 = [sb(f"x1_{i}", [P, T, E]) for i in range(2)]
        x2 = sb("x2", [P, T, E])
        x_out = sb("x_out", [P, T, E])
        xh = sb("xh", [P, T, E])
        lh = sb("lh", [P, T, HD])
        stats = [sb(f"stats{i}", [P, T, 6]) for i in range(3)]
        mv = [sb(f"mv{i}", [P, T, 2]) for i in range(3)]
        veps = [sb(f"veps{i}", [P, T]) for i in range(3)]
        rstd = [sb(f"rstd{i}", [P, T]) for i in range(3)]
        xT = sb("xT", [P, C, S])
        leftT = sb("leftT", [P, S])
        qp = sb("qp", [P, PARTS, S], BF16)
        kp = sb("kp", [P, PARTS, S], BF16)
        rest = sb("rest", [P, S])
        sq_q = sb("sq_q", [P, S], BF16)
        sq_k = sb("sq_k", [P, S], BF16)
        QS = [sb(f"QS{i}", [P, H, S], BF16) for i in range(2)]
        KS = [sb(f"KS{i}", [P, H, S], BF16) for i in range(2)]
        VS = [sb(f"VS{i}", [P, T, H, COL]) for i in range(2)]
        probs = [sb(f"probs{i}", [P, 2, S]) for i in range(PRING)]
        ot_t = sb("ot_t", [P, S // 32, 32])
        recip = sb("recip", [P, S // 32, 2])
        on = sb("on", [P, S // 32, 32])
        otn = [sb(f"otn{g}", [P, S]) for g in range(2)]
        norms = sb("norms", [64, 1])
        norm_row = sb("norm_row", [1, 64])
        norm_prod = sb("norm_prod", [1, H])
        worst = sb("worst", [1, 1])
        safe = sb("safe", [1, 1], I32)
        neg_max = sb("neg_max", [P, T, H])
        shift = sb("shift", [H, PARTS, S], BF16)
        shift_rest = sb("shift_rest", [H, S])
        ones_row = sb("ones_row", [H, S], BF16)

        scores = [ctx.enter_context(nc.psum_tensor(f"scores{i}", [P, 2, S], F32)) for i in range(2)]
        ot = [ctx.enter_context(nc.psum_tensor(f"ot{i}", [P, S], F32)) for i in range(2)]
        misc = [ctx.enter_context(nc.psum_tensor(f"misc{i}", [P, S], F32)) for i in range(2)]

        spec_loaded = sem("spec_loaded")
        small_loaded = sem("small_loaded")
        x_loaded = [sem(f"x_loaded{i}") for i in range(2)]
        ones_set = sem("ones_set")
        ks_ones = sem("ks_ones")
        consts_set = sem("consts_set")
        bias_set = sem("bias_set")
        nsin_set = sem("nsin_set")
        ffn_mm = sem("ffn_mm")
        ffn_copied = sem("ffn_copied")
        misc_ready = sem("misc_ready")
        evacuated = sem("evacuated")
        stats_done = [sem(f"stats_done{i}") for i in range(3)]
        mv_done = [sem(f"mv_done{i}") for i in range(3)]
        veps_done = [sem(f"veps_done{i}") for i in range(3)]
        rstd_done = [sem(f"rstd_done{i}") for i in range(3)]
        normed = [sem(f"normed{i}") for i in range(3)]
        xb_done = sem("xb_done")
        x2b_done = sem("x2b_done")
        qp_step = sem("qp_step")
        kp_step = sem("kp_step")
        sq_done = sem("sq_done")
        q_stored = sem("q_stored")
        k_stored = sem("k_stored")
        qs_loaded = sem("qs_loaded")
        ks_loaded = sem("ks_loaded")
        guard_step = sem("guard_step")
        shift_zero = sem("shift_zero")
        max_ready = sem("max_ready")
        max_used = sem("max_used")
        maxT_ready = sem("maxT_ready")
        shift_step = sem("shift_step")
        shift_ready = sem("shift_ready")
        shift_loaded = sem("shift_loaded")
        scores_ready = sem("scores_ready")
        exp_done = sem("exp_done")
        quad_done = sem("quad_done")
        ot_taken = sem("ot_taken")
        ot_step = sem("ot_step")
        otn_ready = sem("otn_ready")
        out_stored = sem("out_stored")

        block = ctx.enter_context(nc.Block())

        def wait(eng, s, value):
            if static(value) and value <= 0:
                return
            eng.wait_ge(s, value)

        def wait_alone(eng, s, value):
            if not static(value):
                value = eng.to_reg(value)
                eng.wait_ge(ones_set, 1)
            wait(eng, s, value)

        def iterations(eng, body):
            body(0, 0)
            with eng.Fori(1, B - 1, 2) as i:
                body(i, 1)
                body(i + 1, 0)
            body(B - 1, 1)

        def is_first(it):
            return static(it) and it == 0

        def is_last(it):
            return static(it) and it == B - 1

        @block.sync
        def _(sp):
            def load_x(b, par):
                sp.dma_start(x_in[par][:, :, :].rearrange("p t e -> p (t e)"), x_v[b]).then_inc(x_loaded[par], 16)

            def stack_parts(b, par, it):
                wait_alone(sp, evacuated, evac_count("QT", it))
                wait_alone(sp, qs_loaded, 48 * b)
                for i in range(PARTS):
                    sp.dma_start(q_scr[:, i * Dh:(i + 1) * Dh, :], qp[:, i, :]).then_inc(q_stored, 16)
                wait_alone(sp, evacuated, evac_count("KT", it))
                wait_alone(sp, ks_loaded, 16 * b)
                for j in range(PARTS):
                    for i in range(PARTS):
                        r = (PARTS * j + i) * Dh
                        sp.dma_start(k_scr[:, r:r + Dh, :], kp[:, j, :]).then_inc(k_stored, 16)
                wait_alone(sp, quad_done, QUADS * (b - 1))
                wait_alone(sp, q_stored, 48 * (b + 1))
                for j in range(PARTS):
                    r = j * PARTS * Dh
                    sp.dma_start(QS[par][r:r + PARTS * Dh, :, :],
                                 q_scr.rearrange("h r s -> r h s")).then_inc(qs_loaded, 16)
                wait_alone(sp, k_stored, 144 * (b + 1))
                sp.dma_start(KS[par][0:SROW, :, :], k_scr.rearrange("h r s -> r h s")).then_inc(ks_loaded, 16)

            def shift_rows(b, par):
                wait_alone(sp, shift_ready, b + 1)
                for j in range(PARTS):
                    sp.dma_start(QS[par][SROW + j:SROW + j + 1, :, :], shift[:, j, :]).then_inc(shift_loaded, 16)

            def store_out(b, it):
                wait_alone(sp, evacuated, evac_count("F2b", it))
                sp.dma_start(out_v[b], x_out[:, :, :].rearrange("p t e -> p (t e)")).then_inc(out_stored, 16)

            sp.sem_inc(out_stored, 16)
            load_x(0, 0)
            sp.dma_start(wre_sb[:, :, :], w_re.rearrange("(c p) e -> p c e", p=P)).then_inc(spec_loaded, 16)
            sp.dma_start(wim_sb[:, :, :], w_im.rearrange("(c p) e -> p c e", p=P)).then_inc(spec_loaded, 16)
            sp.dma_start(bias_raw[:, :], bias.partition_broadcast(P)).then_inc(small_loaded, 16)
            load_x(1, 1)
            sp.dma_start(wo_sb[:, :, :], wo_rows.rearrange("g p e -> p g e")).then_inc(small_loaded, 16)
            sp.wait_ge(ones_set, 1)
            for i in range(2):
                for j in range(PARTS):
                    sp.dma_start(KS[i][SROW + j:SROW + j + 1, :, :], ones_row[:, :]).then_inc(ks_ones, 16)
            stack_parts(0, 0, PROLOGUE)
            shift_rows(0, 0)

            def body(it, par):
                if not (static(it) and it + 2 >= B):
                    wait_alone(sp, evacuated, ring_base(it))
                    load_x(it + 2, par)
                if not is_last(it):
                    stack_parts(it + 1, 1 - par, it)
                if not is_first(it):
                    store_out(it - 1, it)
                if not is_last(it):
                    shift_rows(it + 1, 1 - par)

            body(0, 0)
            with sp.Fori(1, B - 3, 2) as i:
                body(i, 1)
                body(i + 1, 0)
            for it in range(B - 3, B):
                body(it, it % 2)
            store_out(B - 1, EPILOGUE)
            sp.wait_ge(out_stored, 16 * (B + 1))

        @block.gpsimd
        def _(pool):
            nc.gpsimd.memset(ones_row[:, :], 1.0).then_inc(ones_set, 1)
            nc.gpsimd.memset(power[:, :], NORM_POWER).then_inc(consts_set, 1)
            for i in range(2):
                nc.gpsimd.memset(VS[i][:, :, :, :], 0.0).then_inc(consts_set, 1)
            pool.wait_ge(consts_set, 3)
            for i in range(2):
                for par in range(2):
                    nc.gpsimd.memset(VS[i][:, :, par::2, DEN + Dh * par:DEN + Dh * (par + 1)], 1.0).then_inc(consts_set, 1)
            nc.gpsimd.memset(on[:, :, :], 0.0).then_inc(consts_set, 1)
            pool.wait_ge(consts_set, 8)
            nc.gpsimd.memset(on[:, :, DEN:DEN + 1], 1.0).then_inc(consts_set, 1)
            pool.wait_ge(small_loaded, 16 * 7)
            nc.gpsimd.tensor_scalar(half_bias[:, :], bias_raw[:, :], 0.5, None, ALU.mult).then_inc(bias_set, 1)

            def rstd_of(k, b):
                wait_alone(pool, mv_done[k], b + 1)
                nc.gpsimd.tensor_scalar(veps[k][:, :], mv[k][:, :, 1], EPS, None, ALU.add).then_inc(veps_done[k], 1)
                wait(pool, veps_done[k], b + 1)
                nc.gpsimd.tensor_tensor(rstd[k][:, :], veps[k][:, :], power[:, :], ALU.pow).then_inc(rstd_done[k], 1)

            def add_bias(buf, done):
                nc.gpsimd.tensor_tensor(buf[:, :, :], buf[:, :, :],
                                        half_bias[:, :].unsqueeze(1).to_broadcast([P, T, E]), ALU.add).then_inc(done, 1)

            def norm0(b, par):
                rstd_of(0, b)
                wait(pool, normed[0], b + 1)
                add_bias(x_in[par], xb_done)

            def prefix(b):
                rstd_of(1, b)
                for parts, sq, step in ((qp, sq_q, qp_step), (kp, sq_k, kp_step)):
                    wait(pool, step, 3 * b + 1)
                    nc.gpsimd.tensor_tensor(sq[:, :], parts[:, 0, :], parts[:, 0, :], ALU.mult).then_inc(sq_done, 1)

            def suffix_norm(b):
                rstd_of(2, b)
                wait(pool, normed[2], b + 1)
                add_bias(x2, x2b_done)

            pool.wait_ge(bias_set, 1)
            norm0(0, 0)
            prefix(0)
            norm0(1, 1)

            def body(it, par, tail=True):
                if not is_first(it):
                    suffix_norm(it - 1)
                if not is_last(it):
                    prefix(it + 1)
                if tail:
                    norm0(it + 2, par)

            body(0, 0)
            with pool.Fori(1, B - 3, 2) as i:
                body(i, 1)
                body(i + 1, 0)
            for it in range(B - 3, B):
                body(it, it % 2, tail=it + 2 < B)
            suffix_norm(B - 1)

        @block.scalar
        def _(act):
            act.dma_start(cos_sb[:, :, :], cos_tab.rearrange("(c p) e -> p c e", p=P)).then_inc(spec_loaded, 16)
            act.dma_start(sin_sb[:, :, :], sin_tab.rearrange("(c p) e -> p c e", p=P)).then_inc(spec_loaded, 16)
            act.dma_start(ident[:, :], ident_in).then_inc(small_loaded, 16)
            act.dma_start(head_ones[:, :], head_ones_in).then_inc(small_loaded, 16)
            act.dma_start(wq_sb[:, :], wq_t).then_inc(small_loaded, 16)
            act.dma_start(wk_sb[:, :], wk_t).then_inc(small_loaded, 16)
            act.dma_start(wv_sb[:, :], wv_t).then_inc(small_loaded, 16)
            act.wait_ge(spec_loaded, 64)
            nc.scalar.mul(nsin_sb[:, :, :], sin_sb[:, :, :], -1.0).then_inc(nsin_set, 1)
            act.wait_ge(ffn_mm, 1)
            nc.scalar.copy(are_t[:, :, :], scores[0][:, 0, :].rearrange("p (c e) -> p c e", c=C)).then_inc(ffn_copied, 1)
            act.wait_ge(ffn_mm, 2)
            nc.scalar.copy(aim_t[:, :, :], scores[0][:, 1, :].rearrange("p (c e) -> p c e", c=C)).then_inc(ffn_copied, 1)
            act.wait_ge(ffn_mm, 3)
            nc.scalar.mul(half_ffn[:, :, :], scores[1][:, 0, :].rearrange("p (c e) -> p c e", c=C),
                          0.5 / E).then_inc(ffn_copied, 1)

            def body(b, par):
                for u in range(PAIRS):
                    wait(act, scores_ready, PAIRS * b + u + 1)
                    wait(act, quad_done, QUADS * b + (u - PRING) // 2 + 1)
                    nc.scalar.activation(probs[u % PRING][:, :, :], scores[u % 2][:, :, :], ACT.Exp,
                                         scale=SCORE_SCALE).then_inc(exp_done, 1)

            iterations(act, body)

        @block.tensor
        def _(pe):
            mm = nc.tensor.matmul

            pe.wait_ge(spec_loaded, 64)
            for m in range(C):
                o = scores[0][:, 0, m * E:(m + 1) * E]
                for c in range(C):
                    mm(o, wre_sb[:, c, m * P:(m + 1) * P], cos_sb[:, c, :], start=c == 0, stop=False)
                for c in range(C):
                    last = mm(o, wim_sb[:, c, m * P:(m + 1) * P], sin_sb[:, c, :], start=False, stop=c == C - 1)
            last.then_inc(ffn_mm, 1)
            pe.wait_ge(nsin_set, 1)
            for m in range(C):
                o = scores[0][:, 1, m * E:(m + 1) * E]
                for c in range(C):
                    mm(o, wim_sb[:, c, m * P:(m + 1) * P], cos_sb[:, c, :], start=c == 0, stop=False)
                for c in range(C):
                    last = mm(o, wre_sb[:, c, m * P:(m + 1) * P], nsin_sb[:, c, :], start=False, stop=c == C - 1)
            last.then_inc(ffn_mm, 1)
            pe.wait_ge(ffn_copied, 2)
            for m in range(C):
                o = scores[1][:, 0, m * E:(m + 1) * E]
                for c in range(C):
                    mm(o, are_t[:, c, m * P:(m + 1) * P], cos_sb[:, c, :], start=c == 0, stop=False)
                for c in range(C):
                    last = mm(o, aim_t[:, c, m * P:(m + 1) * P], nsin_sb[:, c, :], start=False, stop=c == C - 1)
            last.then_inc(ffn_mm, 1)
            pe.wait_ge(small_loaded, 16 * 7)
            pe.wait_ge(consts_set, 9)

            def job(name, n, base, b, it):
                bank = misc[n % 2]

                def after(done):
                    (wait_alone if name == "NT" else wait)(pe, evacuated, evac_count(done, it))

                wait(pe, evacuated, base + n - 1)
                if name in ("T1a", "T1b", "T3a", "T3b"):
                    c = "ab".index(name[-1])
                    k = 0 if name[1] == "1" else 2
                    wait(pe, normed[k], b + 1)
                    for t in range(T):
                        last = nc.tensor.transpose(bank[:, t * P:(t + 1) * P], xh[:, t, c * P:(c + 1) * P], ident[:, :])
                elif name in ("F1a", "F1b", "F2a", "F2b"):
                    after("T1b" if name[1] == "1" else "T3b")
                    for t in (0, 1) if name[-1] == "a" else (2, 3):
                        for c in range(C):
                            last = mm(bank[:, (t % 2) * E:(t % 2 + 1) * E], xT[:, c, t * P:(t + 1) * P],
                                      half_ffn[:, c, :], start=c == 0, stop=c == C - 1)
                elif name in ("WOa", "WOb"):
                    wait(pe, otn_ready, 2 * (b + 1))
                    for t in (0, 1) if name[-1] == "a" else (2, 3):
                        for g in range(2):
                            last = mm(bank[:, (t % 2) * E:(t % 2 + 1) * E], otn[g][:, t * P:(t + 1) * P],
                                      wo_sb[:, g, :], start=g == 0, stop=g == 1)
                elif name == "LT":
                    wait(pe, normed[1], b + 1)
                    for t in range(T):
                        last = nc.tensor.transpose(bank[:, t * P:(t + 1) * P], lh[:, t, :], ident[:, :])
                elif name in ("QT", "KT"):
                    after("LT")
                    last = mm(bank[:, :], (wq_sb if name == "QT" else wk_sb)[:, :], leftT[:, :], start=True, stop=True)
                elif name == "V":
                    for t in range(T):
                        last = mm(bank[:, t * HD:(t + 1) * HD], leftT[:, t * P:(t + 1) * P], wv_sb[:, :],
                                  start=True, stop=True)
                elif name == "N":
                    wait_alone(pe, sq_done, 2 * (b + 1))
                    mm(bank[0:32, :], head_ones[:, :], sq_q[:, :], start=True, stop=True)
                    last = mm(bank[32:64, :], head_ones[:, :], sq_k[:, :], start=True, stop=True)
                elif name == "NT":
                    after("N")
                    last = mm(bank[0:1, 0:64], norms[:, :], ident[0:64, 0:64], start=True, stop=True)
                last.then_inc(misc_ready, 1)

            def score_pair(b, par, u):
                _, _, kt, heads = quad_units(u // 2)
                wait(pe, exp_done, PAIRS * b + u - 1)
                for i in range(2):
                    h = heads[2 * (u % 2) + i]
                    last = mm(scores[u % 2][:, i, :], KS[par][0:ROWS, h, kt * P:(kt + 1) * P],
                              QS[par][0:ROWS, h, :], start=True, stop=True)
                last.then_inc(scores_ready, 1)

            def rows_ready(b):
                wait(pe, qs_loaded, 48 * (b + 1))
                wait(pe, ks_loaded, 16 * (b + 1))
                wait(pe, shift_loaded, 48 * (b + 1))

            def value_quad(b, par, s):
                g, p, kt, heads = quad_units(s)
                if s == 0:
                    wait(pe, evacuated, ring_base(b))
                if s % 8 == 0:
                    wait(pe, ot_taken, 2 * b + g - 1)
                wait(pe, exp_done, PAIRS * b + 2 * s + 2)
                for j, h in enumerate(heads):
                    last = mm(ot[g][COL * j:COL * (j + 1), :], VS[par][:, kt, h, :],
                              probs[(2 * s + j // 2) % PRING][:, j % 2, :], start=s % 8 == 0, stop=s % 8 == 7)
                last.then_inc(quad_done, 1)

            def maxima(b, par, base):
                wait_alone(pe, guard_step, 3 * (b + 1))
                small = pe.value_load(safe[0:1, 0:1], min_val=0, max_val=1)
                with pe.If(small == 0):
                    wait(pe, evacuated, base)
                    wait(pe, qs_loaded, 48 * (b + 1))
                    wait(pe, ks_loaded, 16 * (b + 1))
                    for h in range(H):
                        for t in range(T):
                            n = h * T + t
                            if n >= 2:
                                wait(pe, max_used, H * T * b + n - 1)
                            mm(misc[n % 2][:, :], QS[par][0:SROW, h, t * P:(t + 1) * P], KS[par][0:SROW, h, :],
                               start=True, stop=True).then_inc(max_ready, 1)
                    wait(pe, max_used, H * T * (b + 1))
                    for t in range(T):
                        last = mm(misc[0][0:H, t * P:(t + 1) * P], neg_max[:, t, :], ident[:, :], start=True, stop=True)
                    last.then_inc(maxT_ready, 1)
                    wait(pe, shift_step, 3 * b + 2)
                with pe.Else():
                    pe.sem_inc(max_ready, H * T)
                    pe.sem_inc(maxT_ready, 1)

            def run_jobs(it, s):
                for n, (at, name) in enumerate(jobs_of(it)):
                    if at == s:
                        b = it + 1 if name in PRE_NAMES else it - 1
                        job(name, n, ring_base(it), b, it)

            pe.wait_ge(ffn_copied, 3)
            for s in range(QUADS):
                run_jobs(PROLOGUE, s)
            maxima(0, 0, ring_base(0))
            rows_ready(0)
            pe.wait_ge(ks_ones, 96)
            score_pair(0, 0, 0)
            score_pair(0, 0, 1)

            def body(it, par):
                for s in range(QUADS):
                    for u in (2 * s + 2, 2 * s + 3):
                        if u < PAIRS:
                            score_pair(it, par, u)
                    if s == QUADS - 1 and not is_last(it):
                        rows_ready(it + 1)
                        score_pair(it + 1, 1 - par, 0)
                        score_pair(it + 1, 1 - par, 1)
                    value_quad(it, par, s)
                    run_jobs(it, s)
                    if s == GUARD_SLOT and not is_last(it):
                        maxima(it + 1, 1 - par, ring_base(it) + len(jobs_of(it)))

            iterations(pe, body)
            for s in range(QUADS):
                run_jobs(EPILOGUE, s)

        @block.vector
        def _(dve):
            def got(n, base):
                wait(dve, misc_ready, base + n + 1)

            def norm_stats(k, src, width, b):
                for t in range(T):
                    last = nc.vector.bn_stats(stats[k][:, t, :], src[:, t, 0:E])
                last.then_inc(stats_done[k], 1)
                wait_alone(dve, stats_done[k], b + 1)
                for t in range(T):
                    last = nc.vector.bn_aggr(mv[k][:, t, :], stats[k][:, t, :])
                last.then_inc(mv_done[k], 1)

            def norm_apply(k, src, dst, width, b):
                wait(dve, rstd_done[k], b + 1)
                for t in range(T):
                    last = nc.vector.tensor_scalar(dst[:, t, 0:width], src[:, t, 0:width], mv[k][:, t, 0:1],
                                                   rstd[k][:, t:t + 1], ALU.subtract, ALU.mult)
                last.then_inc(normed[k], 1)

            def norm0(b, par):
                wait(dve, x_loaded[par], 8 * (b - par) + 16)
                norm_stats(0, x_in[par], E, b)
                norm_apply(0, x_in[par], xh, E, b)

            def split(bank, parts, step, b, stored):
                wait(dve, stored[0], stored[1])
                nc.vector.tensor_copy(parts[:, 0, :], bank[:, :]).then_inc(step, 1)
                wait(dve, step, 3 * b + 1)
                nc.vector.tensor_tensor(rest[:, :], bank[:, :], parts[:, 0, :], ALU.subtract).then_inc(step, 1)
                wait(dve, step, 3 * b + 2)
                nc.vector.tensor_copy(parts[:, 1, :], rest[:, :]).then_inc(step, 1)
                wait(dve, step, 3 * b + 3)
                return nc.vector.tensor_tensor(parts[:, 2, :], rest[:, :], parts[:, 1, :], ALU.subtract)

            def evacuate(name, n, base, b, par):
                bank = misc[n % 2]
                got(n, base)
                if name in ("T1a", "T1b", "T3a", "T3b"):
                    c = "ab".index(name[-1])
                    nc.vector.tensor_copy(xT[:, c, :], bank[:, :]).then_inc(evacuated, 1)
                elif name in ("F1a", "F1b"):
                    t = 0 if name[-1] == "a" else 2
                    wait(dve, xb_done, b + 1)
                    nc.vector.tensor_tensor(x1[par][:, t:t + 2, :], bank[:, :].rearrange("p (t e) -> p t e", t=2),
                                            x_in[par][:, t:t + 2, :], ALU.add).then_inc(evacuated, 1)
                elif name in ("WOa", "WOb"):
                    t = 0 if name[-1] == "a" else 2
                    nc.vector.tensor_tensor(x2[:, t:t + 2, :], bank[:, :].rearrange("p (t e) -> p t e", t=2),
                                            x1[par][:, t:t + 2, :], ALU.add).then_inc(evacuated, 1)
                elif name in ("F2a", "F2b"):
                    t = 0 if name[-1] == "a" else 2
                    wait(dve, x2b_done, b + 1)
                    wait(dve, out_stored, 16 * (b + 1))
                    nc.vector.tensor_tensor(x_out[:, t:t + 2, :], bank[:, :].rearrange("p (t e) -> p t e", t=2),
                                            x2[:, t:t + 2, :], ALU.add).then_inc(evacuated, 1)
                elif name == "LT":
                    nc.vector.tensor_copy(leftT[:, :], bank[:, :]).then_inc(evacuated, 1)
                elif name == "QT":
                    wait(dve, sq_done, 2 * b)
                    split(bank, qp, qp_step, b, (q_stored, 48 * b)).then_inc(evacuated, 1)
                elif name == "KT":
                    split(bank, kp, kp_step, b, (k_stored, 144 * b)).then_inc(evacuated, 1)
                elif name == "V":
                    if not (static(b) and b < 2):
                        wait(dve, quad_done, QUADS * (b - 1))
                    for r in range(2):
                        last = nc.vector.tensor_copy(
                            VS[par][:, :, r::2, Dh * r:Dh * (r + 1)],
                            bank[:, :].rearrange("p (t h r d) -> p t h r d", t=T, r=2, d=Dh)[:, :, :, r, :])
                    last.then_inc(evacuated, 1)
                elif name == "N":
                    nc.vector.reduce_max(norms[:, :], bank[0:64, :], AX.X).then_inc(evacuated, 1)
                elif name == "NT":
                    nc.vector.tensor_copy(norm_row[:, :], bank[0:1, 0:64]).then_inc(evacuated, 1)
                    wait(dve, evacuated, base + n + 1)
                    nc.vector.tensor_tensor(norm_prod[:, :], norm_row[:, 0:H], norm_row[:, 32:32 + H], ALU.mult).then_inc(guard_step, 1)
                    wait(dve, guard_step, 3 * b + 1)
                    nc.vector.reduce_max(worst[:, :], norm_prod[:, :], AX.X).then_inc(guard_step, 1)
                    wait(dve, guard_step, 3 * b + 2)
                    nc.vector.tensor_scalar(safe[:, :], worst[:, :], SAFE_PRODUCT, None, ALU.is_le).then_inc(guard_step, 1)

            def normalize(b, g):
                wait(dve, quad_done, QUADS * b + 8 * (g + 1))
                nc.vector.transpose(ot_t[:, :, :].rearrange("p c r -> p (c r)"), ot[g][:, :]).then_inc(ot_taken, 1)
                wait(dve, ot_taken, 2 * b + g + 1)
                nc.vector.reciprocal(recip[:, :, :], ot_t[:, :, DEN::Dh]).then_inc(ot_step, 1)
                wait(dve, ot_step, 4 * b + 2 * g + 1)
                nc.vector.tensor_tensor(on[:, :, 0:DEN].rearrange("p c (r d) -> p c r d", d=Dh),
                                        ot_t[:, :, 0:DEN].rearrange("p c (r d) -> p c r d", d=Dh),
                                        recip[:, :, :].unsqueeze(3).to_broadcast([P, S // 32, 2, Dh]),
                                        ALU.mult).then_inc(ot_step, 1)
                wait(dve, ot_step, 4 * b + 2 * g + 2)
                nc.vector.transpose(otn[g][:, :], on[:, :, :].rearrange("p c r -> p (c r)")).then_inc(otn_ready, 1)

            def guard(b):
                wait_alone(dve, guard_step, 3 * (b + 1))
                wait_alone(dve, shift_loaded, 48 * b)
                small = dve.value_load(safe[0:1, 0:1], min_val=0, max_val=1)
                with dve.If(small == 0):
                    for n in range(H * T):
                        wait(dve, max_ready, H * T * b + n + 1)
                        nc.vector.tensor_reduce(neg_max[:, n % T, n // T:n // T + 1], misc[n % 2][:, :], AX.X, ALU.max,
                                                negate=True).then_inc(max_used, 1)
                    wait(dve, maxT_ready, b + 1)
                    bank = misc[0][0:H, :]
                    nc.vector.tensor_copy(shift[:, 0, :], bank).then_inc(shift_step, 1)
                    wait(dve, shift_step, 3 * b + 1)
                    nc.vector.tensor_tensor(shift_rest[:, :], bank, shift[:, 0, :], ALU.subtract).then_inc(shift_step, 1)
                    wait(dve, shift_step, 3 * b + 2)
                    nc.vector.tensor_copy(shift[:, 1, :], shift_rest[:, :]).then_inc(shift_step, 1)
                    wait(dve, shift_step, 3 * b + 3)
                    nc.vector.tensor_tensor(shift[:, 2, :], shift_rest[:, :], shift[:, 1, :], ALU.subtract).then_inc(shift_ready, 1)
                with dve.Else():
                    dve.sem_inc(shift_step, 3)
                    dve.sem_inc(max_used, H * T)
                    nc.vector.memset(shift[:, :, :], 0.0).then_inc(shift_ready, 1)

            def run_jobs(it, par, s):
                for n, (at, name) in enumerate(jobs_of(it)):
                    if at != s:
                        continue
                    b = it + 1 if name in PRE_NAMES else it - 1
                    evacuate(name, n, ring_base(it), b, 1 - par)
                    if name == "F1b":
                        wait(dve, evacuated, evac_count(name, it))
                        norm_stats(1, x1[1 - par], HD, b)
                        norm_apply(1, x1[1 - par], lh, HD, b)
                    if name == "WOb":
                        wait(dve, evacuated, evac_count(name, it))
                        norm_stats(2, x2, E, b)
                        norm_apply(2, x2, xh, E, b)

            dve.wait_ge(consts_set, 9)
            norm0(0, 0)
            for s in range(QUADS):
                run_jobs(PROLOGUE, 1, s)
            norm0(1, 1)
            guard(0)

            def body(it, par, tail=True):
                for s in range(QUADS):
                    if s == 0 and not is_first(it):
                        normalize(it - 1, 1)
                    if s == 8:
                        normalize(it, 0)
                    run_jobs(it, par, s)
                    if s == GUARD_SLOT - 1 and tail:
                        norm0(it + 2, par)
                    if s == GUARD_SLOT and not is_last(it):
                        guard(it + 1)

            body(0, 0)
            with dve.Fori(1, B - 3, 2) as i:
                body(i, 1)
                body(i + 1, 0)
            for it in range(B - 3, B):
                body(it, it % 2, tail=it + 2 < B)
            normalize(B - 1, 1)
            for s in range(QUADS):
                run_jobs(EPILOGUE, 0, s)


def kernel(L0_attn_x, L0_attn_Wq, L0_attn_Wk, L0_attn_Wv, L0_attn_Wo, L0_attn_bo,
           L0_ffn_w_freq_real, L0_ffn_w_freq_imag, L0_ffn_bias):
    import numpy as np
    import concourse.bacc as bacc
    from concourse.bass_utils import run_bass_kernel_spmd

    wo_rows = np.zeros((2, P, E), np.float32)
    wo = np.asarray(L0_attn_Wo)
    for h in range(H):
        g, j, par = h // 8, (h % 8) // 2, h % 2
        r = COL * j + Dh * par
        wo_rows[g, r:r + Dh, :] = wo[:, h * Dh:(h + 1) * Dh].T
    wo_rows[0, DEN, :] = np.asarray(L0_attn_bo)

    angle = 2.0 * np.pi * (np.outer(np.arange(E), np.arange(E)) % E) / E
    head_ones = np.zeros((P, 32), np.float32)
    head_ones[np.arange(P), np.arange(P) // Dh] = 1.0

    import ml_dtypes
    arrays = {
        "x": np.ascontiguousarray(L0_attn_x),
        "wq_t": np.ascontiguousarray(np.asarray(L0_attn_Wq).T),
        "wk_t": np.ascontiguousarray(np.asarray(L0_attn_Wk).T),
        "wv_t": np.ascontiguousarray(np.asarray(L0_attn_Wv).T),
        "wo_rows": wo_rows,
        "w_re": np.ascontiguousarray(L0_ffn_w_freq_real),
        "w_im": np.ascontiguousarray(L0_ffn_w_freq_imag),
        "bias": np.ascontiguousarray(L0_ffn_bias),
        "cos_tab": np.cos(angle).astype(np.float32),
        "sin_tab": np.sin(angle).astype(np.float32),
        "ident_in": np.eye(P, dtype=np.float32),
        "head_ones_in": head_ones.astype(ml_dtypes.bfloat16),
    }
    nc = bacc.Bacc("TRN2", target_bir_lowering=False, num_devices=1)
    args = [nc.dram_tensor(n, a.shape, mybir.dt.from_np(a.dtype), kind="ExternalInput").ap()
            for n, a in arrays.items()]
    out = nc.dram_tensor("out", (B, S, E), F32, kind="ExternalOutput").ap()
    build_macaron(nc, *args, out)
    r = run_bass_kernel_spmd(nc, [arrays], core_ids=[0])
    return r.results[0]["out"]
```

```python
import concourse.bass as bass
from concourse import mybir
from contextlib import ExitStack

F32 = mybir.dt.float32
BF16 = mybir.dt.bfloat16
I32 = mybir.dt.int32
ALU = mybir.AluOpType
ACT = mybir.ActivationFunctionType
AX = mybir.AxisListType

B, S, E = 8, 512, 256
H, Dh = 16, 8
HD = H * Dh
P = 128
T = S // P
C = E // P
PARTS = 3
TERMS = PARTS * PARTS
SROW = TERMS * Dh
ROWS = SROW + PARTS
EPS = 1e-5
SCORE_SCALE = 1.0 / float(E // H) ** 0.5
SAFE_SCORE = 60.0
SAFE_PRODUCT = (SAFE_SCORE / SCORE_SCALE) ** 2 / 1.05
NORM_POWER = -0.5

QUADS = 16
PAIRS = 2 * QUADS
PRING = 4
COL = 32
DEN = 2 * Dh

PREFIX = {0: ["T1_0", "T1_1"], 1: ["F1_0", "F1_1"], 2: ["F1_2", "F1_3"], 4: ["LT"], 5: ["KT"], 6: ["QT"],
          7: ["V"], 8: ["N"], 9: ["NT"]}
SUFFIX = {3: ["WO_0"], 4: ["WO_1"], 5: ["WO_2"], 6: ["WO_3"], 10: ["T3_0"], 11: ["T3_1"],
          12: ["F2_0"], 13: ["F2_1"], 14: ["F2_2"], 15: ["F2_3"]}
GUARD_SLOT = 10
NORM0_SLOT = 11
NPRE = sum(len(v) for v in PREFIX.values())
NSUF = sum(len(v) for v in SUFFIX.values())


PRE_NAMES = [n for v in PREFIX.values() for n in v]
PROLOGUE, EPILOGUE = -1, B


def static(v):
    return isinstance(v, int)


def ring_base(it):
    if static(it) and it <= 0:
        return 0 if it == PROLOGUE else NPRE
    if static(it) and it == EPILOGUE:
        return ring_base(B - 1) + NSUF
    return it * (NPRE + NSUF) + (NPRE - NSUF)


def jobs_of(it):
    pre = not (static(it) and it >= B - 1)
    suf = not (static(it) and it <= 0)
    return [(s, name) for s in range(QUADS)
            for name in (SUFFIX.get(s, []) if suf else []) + (PREFIX.get(s, []) if pre else [])]


def evac_count(name, it):
    return ring_base(it) + [n for _, n in jobs_of(it)].index(name) + 1


def quad_units(s):
    g, par, kt = s // 8, (s % 8) // 4, s % 4
    return g, par, kt, [8 * g + 2 * j + par for j in range(4)]


def build_macaron(nc, x, wq_t, wk_t, wv_t, wo_rows, bo, w_re, w_im, bias, cos_tab, sin_tab, ident_in,
                  head_ones_in, out):
    x_v = x.rearrange("b (p t) e -> b p (t e)", t=T)
    out_v = out.rearrange("b (p t) e -> b p (t e)", t=T)

    q_scr = nc.dram_tensor("q_scr", [HD, PARTS, S], BF16, kind="Internal").ap()
    k_scr = nc.dram_tensor("k_scr", [HD, PARTS, PARTS, S], BF16, kind="Internal").ap()

    ctx = ExitStack()
    with ctx:
        def sb(name, shape, dt=F32):
            return ctx.enter_context(nc.sbuf_tensor(name, shape, dt))

        def sem(name):
            return ctx.enter_context(nc.semaphore(name))

        ident = sb("ident", [P, P])
        head_ones = sb("head_ones", [P, 32], BF16)
        cos_sb = sb("cos_sb", [P, C, E])
        sin_sb = sb("sin_sb", [P, C, E])
        nsin_sb = sb("nsin_sb", [P, C, E])
        wre_sb = sb("wre_sb", [P, C, E])
        wim_sb = sb("wim_sb", [P, C, E])
        are_t = sb("are_t", [P, C, E])
        aim_t = sb("aim_t", [P, C, E])
        half_ffn = sb("half_ffn", [P, C, E])
        wq_sb = sb("wq_sb", [P, HD])
        wk_sb = sb("wk_sb", [P, HD])
        wv_sb = sb("wv_sb", [P, HD])
        wo_sb = sb("wo_sb", [P, E])
        bo_sb = sb("bo_sb", [P, E])
        bias_raw = sb("bias_raw", [P, E])
        half_bias = sb("half_bias", [P, E])
        power = sb("power", [P, T])
        x_in = [sb(f"x_in{i}", [P, T, E]) for i in range(2)]
        x1 = [sb(f"x1_{i}", [P, T, E]) for i in range(2)]
        x2 = sb("x2", [P, T, E])
        x_out = sb("x_out", [P, T, E])
        xh = sb("xh", [P, T, E])
        lh = sb("lh", [P, T, HD])
        stats = [sb(f"stats{i}", [P, T, 6]) for i in range(3)]
        mv = [sb(f"mv{i}", [P, T, 2]) for i in range(3)]
        veps = [sb(f"veps{i}", [P, T]) for i in range(3)]
        rstd = [sb(f"rstd{i}", [P, T]) for i in range(3)]
        xT = sb("xT", [P, T, C, P])
        leftT = sb("leftT", [P, S])
        qp = sb("qp", [P, PARTS, S], BF16)
        kp = sb("kp", [P, PARTS, S], BF16)
        rest = sb("rest", [P, S])
        sq_q = sb("sq_q", [P, S], BF16)
        sq_k = sb("sq_k", [P, S], BF16)
        QS = [sb(f"QS{i}", [P, H, S], BF16) for i in range(2)]
        KS = [sb(f"KS{i}", [P, H, S], BF16) for i in range(2)]
        VS = [sb(f"VS{i}", [P, T, H, COL]) for i in range(2)]
        probs = [sb(f"probs{i}", [P, 2, S]) for i in range(PRING)]
        ot_t = sb("ot_t", [P, S // 32, 32])
        recip = sb("recip", [P, S // 32, 2])
        on = sb("on", [P, S // 32, 32])
        otn = sb("otn", [P, S])
        norms = sb("norms", [64, 1])
        norm_row = sb("norm_row", [1, 64])
        norm_prod = sb("norm_prod", [1, H])
        worst = sb("worst", [1, 1])
        safe = sb("safe", [1, 1], I32)
        neg_max = sb("neg_max", [P, T, H])
        shift = sb("shift", [H, PARTS, S], BF16)
        shift_rest = sb("shift_rest", [H, S])
        ones_row = sb("ones_row", [P, S], BF16)

        scores = [ctx.enter_context(nc.psum_tensor(f"scores{i}", [P, 2, S], F32)) for i in range(2)]
        ot = [ctx.enter_context(nc.psum_tensor(f"ot{i}", [P, S], F32)) for i in range(2)]
        misc = [ctx.enter_context(nc.psum_tensor(f"misc{i}", [P, S], F32)) for i in range(2)]

        re_loaded = sem("re_loaded")
        im_loaded = sem("im_loaded")
        ident_loaded = sem("ident_loaded")
        small_loaded = sem("small_loaded")
        x_loaded = [sem(f"x_loaded{i}") for i in range(2)]
        ones_set = sem("ones_set")
        ks_ones = sem("ks_ones")
        consts_set = sem("consts_set")
        bias_set = sem("bias_set")
        nsin_set = sem("nsin_set")
        ffn_mm = sem("ffn_mm")
        ffn_copied = sem("ffn_copied")
        misc_ready = sem("misc_ready")
        evacuated = sem("evacuated")
        stats_done = [sem(f"stats_done{i}") for i in range(3)]
        mv_done = [sem(f"mv_done{i}") for i in range(3)]
        veps_done = [sem(f"veps_done{i}") for i in range(3)]
        rstd_done = [sem(f"rstd_done{i}") for i in range(3)]
        normed = [sem(f"normed{i}") for i in range(3)]
        xb_done = sem("xb_done")
        x2b_done = sem("x2b_done")
        qp_step = sem("qp_step")
        kp_step = sem("kp_step")
        sq_done = sem("sq_done")
        x2_begun = sem("x2_begun")
        q_stored = [sem(f"q_stored{g}") for g in range(2)]
        k_stored = [sem(f"k_stored{g}") for g in range(2)]
        rows_loaded = [sem(f"rows_loaded{g}") for g in range(2)]
        guard_step = sem("guard_step")
        shift_zero = sem("shift_zero")
        max_ready = sem("max_ready")
        max_used = sem("max_used")
        maxT_ready = sem("maxT_ready")
        shift_step = sem("shift_step")
        shift_ready = sem("shift_ready")
        shift_loaded = sem("shift_loaded")
        scores_ready = sem("scores_ready")
        exp_done = sem("exp_done")
        quad_done = sem("quad_done")
        ot_taken = sem("ot_taken")
        ot_step = sem("ot_step")
        otn_ready = sem("otn_ready")
        out_stored = sem("out_stored")

        block = ctx.enter_context(nc.Block())

        def wait(eng, s, value):
            if static(value) and value <= 0:
                return
            eng.wait_ge(s, value)

        def wait_alone(eng, s, value):
            if not static(value):
                value = eng.to_reg(value)
                eng.wait_ge(ones_set, 1)
            wait(eng, s, value)

        def iterations(eng, body):
            body(0, 0)
            with eng.Fori(1, B - 1, 2) as i:
                body(i, 1)
                body(i + 1, 0)
            body(B - 1, 1)

        def is_first(it):
            return static(it) and it == 0

        def is_last(it):
            return static(it) and it == B - 1

        @block.sync
        def _(sp):
            def load_x(b, par):
                sp.dma_start(x_in[par][:, :, :].rearrange("p t e -> p (t e)"), x_v[b]).then_inc(x_loaded[par], 16)

            def stack_parts(b, par, it):
                halves = [(g, slice(64 * g, 64 * (g + 1)), slice(8 * g, 8 * (g + 1))) for g in range(2)]
                for g, half, heads in halves:
                    wait_alone(sp, kp_step, 3 * (b + 1))
                    wait_alone(sp, rows_loaded[g], 64 * b)
                    sp.dma_start(k_scr[half].rearrange("r i j s -> r i (j s)"),
                                 kp[half, :, :].rearrange("r j s -> r (j s)").unsqueeze(1)
                                 .to_broadcast([64, PARTS, PARTS * S])).then_inc(k_stored[g], 16)
                    wait_alone(sp, qp_step, 3 * (b + 1))
                    sp.dma_start(q_scr[half], qp[half, :, :]).then_inc(q_stored[g], 16)
                    wait_alone(sp, quad_done, QUADS * (b - 1))
                    wait_alone(sp, k_stored[g], 16 * (b + 1))
                    sp.dma_start(KS[par][0:SROW, heads, :],
                                 k_scr[half].rearrange("(h d) i j s -> (d i j) h s", d=Dh)).then_inc(rows_loaded[g], 16)
                    wait_alone(sp, q_stored[g], 16 * (b + 1))
                    for j in range(PARTS):
                        sp.dma_start(QS[par][j:SROW:PARTS, heads, :],
                                     q_scr[half].rearrange("(h d) i s -> (d i) h s", d=Dh)).then_inc(rows_loaded[g], 16)

            def shift_rows(b, par):
                wait_alone(sp, shift_ready, b + 1)
                for j in range(PARTS):
                    sp.dma_start(QS[par][SROW + j:SROW + j + 1, :, :], shift[:, j, :]).then_inc(shift_loaded, 16)

            def store_out(b, it):
                for i in range(2):
                    wait_alone(sp, evacuated, evac_count(f"F2_{2 * i + 1}", it))
                    sp.dma_start(out_v[b][:, 2 * i * E:2 * (i + 1) * E],
                                 x_out[:, 2 * i:2 * i + 2, :].rearrange("p t e -> p (t e)")).then_inc(out_stored, 16)

            sp.sem_inc(out_stored, 32)
            sp.dma_start(wre_sb[:, :, :], w_re.rearrange("(c p) e -> p c e", p=P)).then_inc(re_loaded, 16)
            sp.dma_start(wim_sb[:, :, :], w_im.rearrange("(c p) e -> p c e", p=P)).then_inc(im_loaded, 16)
            load_x(0, 0)
            sp.dma_start(bias_raw[:, :], bias.partition_broadcast(P)).then_inc(small_loaded, 16)
            sp.dma_start(bo_sb[:, :], bo.partition_broadcast(P)).then_inc(small_loaded, 16)
            sp.dma_start(wo_sb[:, :], wo_rows).then_inc(small_loaded, 16)
            load_x(1, 1)
            sp.wait_ge(ones_set, 1)
            for i in range(2):
                for j in range(PARTS):
                    sp.dma_start(KS[i][SROW + j:SROW + j + 1, :, :], ones_row[0:H, :]).then_inc(ks_ones, 16)
            stack_parts(0, 0, PROLOGUE)

            def body(it, par):
                if not (static(it) and it + 2 >= B):
                    wait_alone(sp, evacuated, ring_base(it))
                    load_x(it + 2, par)
                if not is_last(it):
                    stack_parts(it + 1, 1 - par, it)
                    shift_rows(it + 1, 1 - par)
                if not is_first(it):
                    store_out(it - 1, it)

            body(0, 0)
            with sp.Fori(1, B - 3, 2) as i:
                body(i, 1)
                body(i + 1, 0)
            for it in range(B - 3, B):
                body(it, it % 2)
            store_out(B - 1, EPILOGUE)
            sp.wait_ge(out_stored, 32 * (B + 1))

        @block.gpsimd
        def _(pool):
            nc.gpsimd.memset(ones_row[:, :], 1.0).then_inc(ones_set, 1)
            nc.gpsimd.memset(power[:, :], NORM_POWER).then_inc(consts_set, 1)
            for i in range(2):
                nc.gpsimd.memset(VS[i][:, :, :, :], 0.0).then_inc(consts_set, 1)
            pool.wait_ge(consts_set, 3)
            for i in range(2):
                for par in range(2):
                    nc.gpsimd.memset(VS[i][:, :, par::2, DEN + Dh * par:DEN + Dh * (par + 1)], 1.0).then_inc(consts_set, 1)

            def rstd_of(k, b):
                wait_alone(pool, mv_done[k], b + 1)
                nc.gpsimd.tensor_scalar(veps[k][:, :], mv[k][:, :, 1], EPS, None, ALU.add).then_inc(veps_done[k], 1)
                wait(pool, veps_done[k], b + 1)
                nc.gpsimd.tensor_tensor(rstd[k][:, :], veps[k][:, :], power[:, :], ALU.pow).then_inc(rstd_done[k], 1)

            def add_bias(buf, done):
                nc.gpsimd.tensor_tensor(buf[:, :, :], buf[:, :, :],
                                        half_bias[:, :].unsqueeze(1).to_broadcast([P, T, E]), ALU.add).then_inc(done, 1)

            def norm0(b, par):
                rstd_of(0, b)
                wait(pool, normed[0], b + 1)
                add_bias(x_in[par], xb_done)

            def square(parts, sq, step, b):
                wait(pool, step, 3 * b + 1)
                nc.gpsimd.tensor_tensor(sq[:, :], parts[:, 0, :], parts[:, 0, :], ALU.mult).then_inc(sq_done, 1)

            def bias_x2(b):
                wait(pool, normed[2], b + 1)
                add_bias(x2, x2b_done)

            rstd_of(0, 0)
            pool.wait_ge(small_loaded, 16 * 7)
            nc.gpsimd.tensor_scalar(half_bias[:, :], bias_raw[:, :], 0.5, None, ALU.mult).then_inc(bias_set, 1)
            pool.wait_ge(bias_set, 1)
            pool.wait_ge(normed[0], 1)
            add_bias(x_in[0], xb_done)
            rstd_of(1, 0)
            square(kp, sq_k, kp_step, 0)
            square(qp, sq_q, qp_step, 0)
            norm0(1, 1)

            def body(it, par, tail=True):
                if not is_last(it):
                    rstd_of(1, it + 1)
                    square(kp, sq_k, kp_step, it + 1)
                if not is_first(it):
                    rstd_of(2, it - 1)
                if not is_last(it):
                    square(qp, sq_q, qp_step, it + 1)
                if not is_first(it):
                    bias_x2(it - 1)
                if tail:
                    norm0(it + 2, par)

            body(0, 0)
            with pool.Fori(1, B - 3, 2) as i:
                body(i, 1)
                body(i + 1, 0)
            for it in range(B - 3, B):
                body(it, it % 2, tail=it + 2 < B)
            rstd_of(2, B - 1)
            bias_x2(B - 1)

        @block.scalar
        def _(act):
            act.dma_start(cos_sb[:, :, :], cos_tab.rearrange("(c p) e -> p c e", p=P)).then_inc(re_loaded, 16)
            act.dma_start(sin_sb[:, :, :], sin_tab.rearrange("(c p) e -> p c e", p=P)).then_inc(im_loaded, 16)
            act.dma_start(ident[:, :], ident_in).then_inc(ident_loaded, 16)
            act.dma_start(head_ones[:, :], head_ones_in).then_inc(small_loaded, 16)
            act.dma_start(wq_sb[:, :], wq_t).then_inc(small_loaded, 16)
            act.dma_start(wk_sb[:, :], wk_t).then_inc(small_loaded, 16)
            act.dma_start(wv_sb[:, :], wv_t).then_inc(small_loaded, 16)
            act.wait_ge(im_loaded, 32)
            nc.scalar.mul(nsin_sb[:, :, :], sin_sb[:, :, :], -1.0).then_inc(nsin_set, 1)
            act.wait_ge(ffn_mm, 1)
            nc.scalar.copy(are_t[:, :, :], scores[0][:, :, 0:E]).then_inc(ffn_copied, 1)
            act.wait_ge(ffn_mm, 2)
            nc.scalar.copy(aim_t[:, :, :], scores[1][:, :, 0:E]).then_inc(ffn_copied, 1)
            act.wait_ge(ffn_mm, 3)
            nc.scalar.mul(half_ffn[:, :, :], scores[0][:, :, 0:E],
                          0.5 / E).then_inc(ffn_copied, 1)

            act.wait_ge(shift_ready, 1)
            for j in range(PARTS):
                act.dma_start(QS[0][SROW + j:SROW + j + 1, :, :], shift[:, j, :]).then_inc(shift_loaded, 16)

            def body(b, par):
                for u in range(PAIRS):
                    wait(act, scores_ready, PAIRS * b + u + 1)
                    wait(act, quad_done, QUADS * b + (u - PRING) // 2 + 1)
                    nc.scalar.activation(probs[u % PRING][:, :, :], scores[u % 2][:, :, :], ACT.Exp,
                                         scale=SCORE_SCALE).then_inc(exp_done, 1)

            iterations(act, body)

        @block.tensor
        def _(pe):
            mm = nc.tensor.matmul

            def spectral(o, k, lhsT, rhs):
                for m in range(C):
                    for c in range(C):
                        last = mm(o[:, m, 0:E], lhsT[:, c, m * P:(m + 1) * P], rhs[:, c, :],
                                  start=(k, c) == (0, 0), stop=(k, c) == (1, C - 1))
                return last

            def keep_awake(n):
                for _ in range(n):
                    mm(ot[1][:, :], ones_row[:, 0:P], ones_row[:, :], start=True, stop=True)

            pe.wait_ge(ones_set, 1)
            keep_awake(7)
            pe.wait_ge(re_loaded, 32)
            spectral(scores[0], 0, wre_sb, cos_sb)
            pe.wait_ge(im_loaded, 32)
            spectral(scores[0], 1, wim_sb, sin_sb).then_inc(ffn_mm, 1)
            spectral(scores[1], 0, wim_sb, cos_sb)
            pe.wait_ge(nsin_set, 1)
            spectral(scores[1], 1, wre_sb, nsin_sb).then_inc(ffn_mm, 1)

            def job(name, n, base, b, it):
                bank = misc[n % 2]

                def after(done):
                    (wait_alone if name == "NT" else wait)(pe, evacuated, evac_count(done, it))

                (wait_alone if name in ("N", "NT") else wait)(pe, evacuated, base + n - 1)
                kind, i = name[:2], int(name[-1]) if "_" in name else 0
                if kind in ("T1", "T3"):
                    wait(pe, normed[0 if kind == "T1" else 2], b + 1)
                    for t in range(2):
                        for c in range(C):
                            last = nc.tensor.transpose(bank[:, (C * t + c) * P:(C * t + c + 1) * P],
                                                       xh[:, 2 * i + t, c * P:(c + 1) * P], ident[:, :])
                elif kind in ("F1", "F2"):
                    after(("T1" if kind == "F1" else "T3") + f"_{i // 2}")
                    for c in range(C):
                        last = mm(bank[:, 0:E], xT[:, i, c, :], half_ffn[:, c, :], start=c == 0, stop=c == C - 1)
                elif kind == "WO":
                    wait(pe, otn_ready, b + 1)
                    last = mm(bank[:, 0:E], otn[:, i * P:(i + 1) * P], wo_sb[:, :], start=True, stop=True)
                elif name == "LT":
                    wait(pe, normed[1], b + 1)
                    for t in range(T):
                        last = nc.tensor.transpose(bank[:, t * P:(t + 1) * P], lh[:, t, :], ident[:, :])
                elif name in ("QT", "KT"):
                    after("LT")
                    last = mm(bank[:, :], (wq_sb if name == "QT" else wk_sb)[:, :], leftT[:, :], start=True, stop=True)
                elif name == "V":
                    for t in range(T):
                        last = mm(bank[:, t * HD:(t + 1) * HD], leftT[:, t * P:(t + 1) * P], wv_sb[:, :],
                                  start=True, stop=True)
                elif name == "N":
                    wait_alone(pe, sq_done, 2 * (b + 1))
                    mm(bank[0:32, :], head_ones[:, :], sq_q[:, :], start=True, stop=True)
                    last = mm(bank[32:64, :], head_ones[:, :], sq_k[:, :], start=True, stop=True)
                elif name == "NT":
                    after("N")
                    last = mm(bank[0:1, 0:64], norms[:, :], ident[0:64, 0:64], start=True, stop=True)
                last.then_inc(misc_ready, 1)

            def score_pair(b, par, u):
                g, _, kt, heads = quad_units(u // 2)
                if u in (0, PAIRS // 2):
                    rows_ready(b, g)
                wait(pe, exp_done, PAIRS * b + u - 1)
                for i in range(2):
                    h = heads[2 * (u % 2) + i]
                    last = mm(scores[u % 2][:, i, :], KS[par][0:ROWS, h, kt * P:(kt + 1) * P],
                              QS[par][0:ROWS, h, :], start=True, stop=True)
                last.then_inc(scores_ready, 1)

            def rows_ready(b, g):
                wait(pe, rows_loaded[g], 64 * (b + 1))
                if g == 0:
                    wait(pe, shift_loaded, 48 * (b + 1))

            def value_quad(b, par, s):
                g, p, kt, heads = quad_units(s)
                if s == 0:
                    wait(pe, evacuated, ring_base(b))
                if s % 8 == 0:
                    wait(pe, ot_taken, 2 * b + g - 1)
                wait(pe, exp_done, PAIRS * b + 2 * s + 2)
                for j, h in enumerate(heads):
                    last = mm(ot[g][COL * j:COL * (j + 1), :], VS[par][:, kt, h, :],
                              probs[(2 * s + j // 2) % PRING][:, j % 2, :], start=s % 8 == 0, stop=s % 8 == 7)
                last.then_inc(quad_done, 1)

            def maxima(b, par, base):
                wait_alone(pe, guard_step, 3 * (b + 1))
                small = pe.value_load(safe[0:1, 0:1], min_val=0, max_val=1)
                with pe.If(small == 0):
                    wait(pe, evacuated, base)
                    wait(pe, rows_loaded[0], 64 * (b + 1))
                    wait(pe, rows_loaded[1], 64 * (b + 1))
                    for h in range(H):
                        for t in range(T):
                            n = h * T + t
                            if n >= 2:
                                wait(pe, max_used, H * T * b + n - 1)
                            mm(misc[n % 2][:, :], QS[par][0:SROW, h, t * P:(t + 1) * P], KS[par][0:SROW, h, :],
                               start=True, stop=True).then_inc(max_ready, 1)
                    wait(pe, max_used, H * T * (b + 1))
                    for t in range(T):
                        last = mm(misc[0][0:H, t * P:(t + 1) * P], neg_max[:, t, :], ident[:, :], start=True, stop=True)
                    last.then_inc(maxT_ready, 1)
                    wait(pe, shift_step, 3 * b + 2)
                with pe.Else():
                    pe.sem_inc(max_ready, H * T)
                    pe.sem_inc(maxT_ready, 1)

            def run_jobs(it, s):
                for n, (at, name) in enumerate(jobs_of(it)):
                    if at == s:
                        b = it + 1 if name in PRE_NAMES else it - 1
                        job(name, n, ring_base(it), b, it)

            pe.wait_ge(ident_loaded, 16)
            run_jobs(PROLOGUE, 0)
            pe.wait_ge(ffn_copied, 2)
            spectral(scores[0], 0, are_t, cos_sb)
            spectral(scores[0], 1, aim_t, nsin_sb).then_inc(ffn_mm, 1)
            pe.wait_ge(ffn_copied, 3)
            pe.wait_ge(small_loaded, 16 * 7)
            pe.wait_ge(consts_set, 7)
            for s in range(1, QUADS):
                run_jobs(PROLOGUE, s)
                if s == 2:
                    keep_awake(16)
            keep_awake(8)
            maxima(0, 0, ring_base(0))
            keep_awake(12)
            pe.wait_ge(ks_ones, 96)
            score_pair(0, 0, 0)
            score_pair(0, 0, 1)

            def body(it, par):
                for s in range(QUADS):
                    for u in (2 * s + 2, 2 * s + 3):
                        if u < PAIRS:
                            score_pair(it, par, u)
                    if s == QUADS - 1 and not is_last(it):
                        score_pair(it + 1, 1 - par, 0)
                        score_pair(it + 1, 1 - par, 1)
                    value_quad(it, par, s)
                    if s == GUARD_SLOT + 1 and not is_last(it):
                        maxima(it + 1, 1 - par, ring_base(it) + len([n for at, n in jobs_of(it) if at <= GUARD_SLOT]))
                    run_jobs(it, s)

            iterations(pe, body)
            for s in range(QUADS):
                run_jobs(EPILOGUE, s)

        @block.vector
        def _(dve):
            def got(n, base):
                wait(dve, misc_ready, base + n + 1)

            def norm_stats(k, src, t):
                ins = nc.vector.bn_stats(stats[k][:, t, :], src[:, t, :])
                if t == T - 1:
                    ins.then_inc(stats_done[k], 1)

            def norm_moments(k, b):
                wait_alone(dve, stats_done[k], b + 1)
                for t in range(T):
                    last = nc.vector.bn_aggr(mv[k][:, t, :], stats[k][:, t, :])
                last.then_inc(mv_done[k], 1)

            def norm_apply(k, src, dst, width, b):
                wait(dve, rstd_done[k], b + 1)
                for t in range(T):
                    last = nc.vector.tensor_scalar(dst[:, t, 0:width], src[:, t, 0:width], mv[k][:, t, 0:1],
                                                   rstd[k][:, t:t + 1], ALU.subtract, ALU.mult)
                last.then_inc(normed[k], 1)

            def norm0(b, par):
                wait(dve, x_loaded[par], 8 * (b - par) + 16)
                for t in range(T):
                    norm_stats(0, x_in[par], t)
                norm_moments(0, b)
                norm_apply(0, x_in[par], xh, E, b)

            def split(bank, parts, step, b, count):
                wait(dve, rows_loaded[0], 64 * b)
                wait(dve, rows_loaded[1], 64 * b)
                nc.vector.tensor_copy(parts[:, 0, :], bank[:, :]).then_inc(step, 1)
                wait(dve, step, 3 * b + 1)
                nc.vector.tensor_tensor(rest[:, :], bank[:, :], parts[:, 0, :], ALU.subtract).then_inc(evacuated, 1)
                wait(dve, evacuated, count)
                nc.vector.tensor_copy(parts[:, 1, :], rest[:, :]).then_inc(step, 1)
                wait(dve, step, 3 * b + 2)
                nc.vector.tensor_tensor(parts[:, 2, :], rest[:, :], parts[:, 1, :], ALU.subtract).then_inc(step, 1)

            def evacuate(name, n, base, b, par):
                bank = misc[n % 2]
                got(n, base)
                kind, i = name[:2], int(name[-1]) if "_" in name else 0
                tile = bank[:, 0:E]
                if kind in ("T1", "T3"):
                    nc.vector.tensor_copy(xT[:, 2 * i:2 * i + 2, :, :],
                                          bank[:, :].rearrange("p (t c q) -> p t c q", t=2, c=C)).then_inc(evacuated, 1)
                elif kind == "F1":
                    wait(dve, xb_done, b + 1)
                    wait(dve, x2_begun, b - 1)
                    nc.vector.tensor_tensor(x1[par][:, i, :], tile, x_in[par][:, i, :], ALU.add).then_inc(evacuated, 1)
                elif kind == "WO":
                    wait(dve, x2_begun, b + 1)
                    nc.vector.tensor_tensor(x2[:, i, :], tile, x2[:, i, :], ALU.add).then_inc(evacuated, 1)
                elif kind == "F2":
                    wait(dve, x2b_done, b + 1)
                    wait(dve, out_stored, 32 * (b + 1))
                    nc.vector.tensor_tensor(x_out[:, i, :], tile, x2[:, i, :], ALU.add).then_inc(evacuated, 1)
                elif name == "LT":
                    nc.vector.tensor_copy(leftT[:, :], bank[:, :]).then_inc(evacuated, 1)
                elif name == "QT":
                    split(bank, qp, qp_step, b, base + n + 1)
                elif name == "KT":
                    wait(dve, sq_done, 2 * b)
                    split(bank, kp, kp_step, b, base + n + 1)
                elif name == "V":
                    if not (static(b) and b < 2):
                        wait(dve, quad_done, QUADS * (b - 1))
                    for r in range(2):
                        last = nc.vector.tensor_copy(
                            VS[par][:, :, r::2, Dh * r:Dh * (r + 1)],
                            bank[:, :].rearrange("p (t h r d) -> p t h r d", t=T, r=2, d=Dh)[:, :, :, r, :])
                    last.then_inc(evacuated, 1)
                elif name == "N":
                    nc.vector.reduce_max(norms[:, :], bank[0:64, :], AX.X).then_inc(evacuated, 1)
                elif name == "NT":
                    nc.vector.tensor_copy(norm_row[:, :], bank[0:1, 0:64]).then_inc(evacuated, 1)
                    wait(dve, evacuated, base + n + 1)
                    nc.vector.tensor_tensor(norm_prod[:, :], norm_row[:, 0:H], norm_row[:, 32:32 + H], ALU.mult).then_inc(guard_step, 1)
                    wait(dve, guard_step, 3 * b + 1)
                    nc.vector.reduce_max(worst[:, :], norm_prod[:, :], AX.X).then_inc(guard_step, 1)
                    wait(dve, guard_step, 3 * b + 2)
                    nc.vector.tensor_scalar(safe[:, :], worst[:, :], SAFE_PRODUCT, None, ALU.is_le).then_inc(guard_step, 1)

            def normalize(b, g):
                wait(dve, quad_done, QUADS * b + 8 * (g + 1))
                nc.vector.transpose(ot_t[:, :, :].rearrange("p c r -> p (c r)"), ot[g][:, :]).then_inc(ot_taken, 1)
                wait(dve, ot_taken, 2 * b + g + 1)
                nc.vector.reciprocal(recip[:, :, :], ot_t[:, :, DEN::Dh]).then_inc(ot_step, 1)
                wait(dve, ot_step, 4 * b + 2 * g + 1)
                wait(dve, otn_ready, b)
                nc.vector.tensor_tensor(on[:, :, DEN * g:DEN * (g + 1)].rearrange("p c (r d) -> p c r d", d=Dh),
                                        ot_t[:, :, 0:DEN].rearrange("p c (r d) -> p c r d", d=Dh),
                                        recip[:, :, :].unsqueeze(3).to_broadcast([P, S // 32, 2, Dh]),
                                        ALU.mult).then_inc(ot_step, 1)
                if g == 1:
                    wait(dve, ot_step, 4 * b + 4)
                    nc.vector.transpose(otn[:, :], on[:, :, :].rearrange("p c r -> p (c r)")).then_inc(otn_ready, 1)

            def begin_x2(par):
                nc.vector.tensor_tensor(x2[:, :, :], x1[par][:, :, :], bo_sb[:, :].unsqueeze(1).to_broadcast([P, T, E]),
                                        ALU.add).then_inc(x2_begun, 1)

            def guard(b):
                wait_alone(dve, guard_step, 3 * (b + 1))
                wait_alone(dve, shift_loaded, 48 * b)
                small = dve.value_load(safe[0:1, 0:1], min_val=0, max_val=1)
                with dve.If(small == 0):
                    for n in range(H * T):
                        wait(dve, max_ready, H * T * b + n + 1)
                        nc.vector.tensor_reduce(neg_max[:, n % T, n // T:n // T + 1], misc[n % 2][:, :], AX.X, ALU.max,
                                                negate=True).then_inc(max_used, 1)
                    wait(dve, maxT_ready, b + 1)
                    bank = misc[0][0:H, :]
                    nc.vector.tensor_copy(shift[:, 0, :], bank).then_inc(shift_step, 1)
                    wait(dve, shift_step, 3 * b + 1)
                    nc.vector.tensor_tensor(shift_rest[:, :], bank, shift[:, 0, :], ALU.subtract).then_inc(shift_step, 1)
                    wait(dve, shift_step, 3 * b + 2)
                    nc.vector.tensor_copy(shift[:, 1, :], shift_rest[:, :]).then_inc(shift_step, 1)
                    wait(dve, shift_step, 3 * b + 3)
                    nc.vector.tensor_tensor(shift[:, 2, :], shift_rest[:, :], shift[:, 1, :], ALU.subtract).then_inc(shift_ready, 1)
                with dve.Else():
                    dve.sem_inc(shift_step, 3)
                    dve.sem_inc(max_used, H * T)
                    nc.vector.memset(shift[:, :, :].bitcast(I32), 0).then_inc(shift_ready, 1)

            def run_jobs(it, par, s):
                for n, (at, name) in enumerate(jobs_of(it)):
                    if at != s:
                        continue
                    b = it + 1 if name in PRE_NAMES else it - 1
                    evacuate(name, n, ring_base(it), b, 1 - par)
                    for kind, k, src in (("F1", 1, x1[1 - par]), ("WO", 2, x2)):
                        if name[:2] != kind:
                            continue
                        i = int(name[-1])
                        for t in ([i - 1] if i else []) + ([i] if i == T - 1 else []):
                            wait(dve, evacuated, evac_count(f"{kind}_{t}", it))
                            norm_stats(k, src, t)
                        if i == T - 1:
                            norm_moments(k, b)
                            if k == 1:
                                norm_apply(k, src, lh, HD, b)
                            elif is_last(it) or (static(it) and it == EPILOGUE):
                                norm_apply(2, x2, xh, E, b)
                if s == 7 and not is_first(it) and not is_last(it) and not (static(it) and it in (PROLOGUE, EPILOGUE)):
                    norm_apply(2, x2, xh, E, it - 1)

            dve.wait_ge(consts_set, 7)
            norm0(0, 0)
            for s in range(QUADS):
                run_jobs(PROLOGUE, 1, s)
            guard(0)
            norm0(1, 1)

            def body(it, par, tail=True):
                for s in range(QUADS):
                    if s == 0 and not is_first(it):
                        normalize(it - 1, 1)
                    run_jobs(it, par, s)
                    if s == 9:
                        normalize(it, 0)
                    if s == 0 and not is_first(it):
                        begin_x2(1 - par)
                    if s == GUARD_SLOT and not is_last(it):
                        guard(it + 1)
                    if s == NORM0_SLOT and tail:
                        norm0(it + 2, par)

            body(0, 0)
            with dve.Fori(1, B - 3, 2) as i:
                body(i, 1)
                body(i + 1, 0)
            for it in range(B - 3, B):
                body(it, it % 2, tail=it + 2 < B)
            normalize(B - 1, 1)
            begin_x2(1)
            for s in range(QUADS):
                run_jobs(EPILOGUE, 0, s)


def kernel(L0_attn_x, L0_attn_Wq, L0_attn_Wk, L0_attn_Wv, L0_attn_Wo, L0_attn_bo,
           L0_ffn_w_freq_real, L0_ffn_w_freq_imag, L0_ffn_bias):
    import numpy as np
    import concourse.bacc as bacc
    from concourse.bass_utils import run_bass_kernel_spmd

    wo_rows = np.zeros((P, E), np.float32)
    wo = np.asarray(L0_attn_Wo)
    for h in range(H):
        g, j, par = h // 8, (h % 8) // 2, h % 2
        r = COL * j + DEN * g + Dh * par
        wo_rows[r:r + Dh, :] = wo[:, h * Dh:(h + 1) * Dh].T

    angle = 2.0 * np.pi * (np.outer(np.arange(E), np.arange(E)) % E) / E
    head_ones = np.zeros((P, 32), np.float32)
    head_ones[np.arange(P), np.arange(P) // Dh] = 1.0

    import ml_dtypes
    arrays = {
        "x": np.ascontiguousarray(L0_attn_x),
        "wq_t": np.ascontiguousarray(np.asarray(L0_attn_Wq).T),
        "wk_t": np.ascontiguousarray(np.asarray(L0_attn_Wk).T),
        "wv_t": np.ascontiguousarray(np.asarray(L0_attn_Wv).T),
        "wo_rows": wo_rows,
        "bo": np.ascontiguousarray(L0_attn_bo),
        "w_re": np.ascontiguousarray(L0_ffn_w_freq_real),
        "w_im": np.ascontiguousarray(L0_ffn_w_freq_imag),
        "bias": np.ascontiguousarray(L0_ffn_bias),
        "cos_tab": np.cos(angle).astype(np.float32),
        "sin_tab": np.sin(angle).astype(np.float32),
        "ident_in": np.eye(P, dtype=np.float32),
        "head_ones_in": head_ones.astype(ml_dtypes.bfloat16),
    }
    nc = bacc.Bacc("TRN2", target_bir_lowering=False, num_devices=1)
    args = [nc.dram_tensor(n, a.shape, mybir.dt.from_np(a.dtype), kind="ExternalInput").ap()
            for n, a in arrays.items()]
    out = nc.dram_tensor("out", (B, S, E), F32, kind="ExternalOutput").ap()
    build_macaron(nc, *args, out)
    r = run_bass_kernel_spmd(nc, [arrays], core_ids=[0])
    return r.results[0]["out"]
```

```python
import concourse.bass as bass
from concourse import mybir
from contextlib import ExitStack

F32 = mybir.dt.float32
BF16 = mybir.dt.bfloat16
I32 = mybir.dt.int32
ALU = mybir.AluOpType
ACT = mybir.ActivationFunctionType
AX = mybir.AxisListType

B, S, E = 8, 512, 256
H, Dh = 16, 8
HD = H * Dh
P = 128
T = S // P
C = E // P
PARTS = 3
TERMS = PARTS * PARTS
SROW = TERMS * Dh
ROWS = SROW + PARTS
EPS = 1e-5
SCORE_SCALE = 1.0 / float(E // H) ** 0.5
SAFE_SCORE = 60.0
SAFE_PRODUCT = (SAFE_SCORE / SCORE_SCALE) ** 2 / 1.05
NORM_POWER = -0.5

QUADS = 16
PAIRS = 2 * QUADS
PRING = 4
COL = 32
DEN = 2 * Dh

PREFIX = {0: ["T1_0", "T1_1"], 1: ["F1_0", "F1_1"], 2: ["F1_2", "F1_3"], 4: ["LT"], 5: ["KT"], 6: ["QT"],
          7: ["V"], 8: ["N"], 9: ["NT"]}
SUFFIX = {3: ["WO_0"], 4: ["WO_1"], 5: ["WO_2"], 6: ["WO_3"], 10: ["T3_0"], 11: ["T3_1"],
          12: ["F2_0"], 13: ["F2_1"], 14: ["F2_2"], 15: ["F2_3"]}
GUARD_SLOT = 10
NORM0_SLOT = 11
NPRE = sum(len(v) for v in PREFIX.values())
NSUF = sum(len(v) for v in SUFFIX.values())

FIRST = [(0, "T1_0", 0), (0, "T1_1", 0), (1, "F1_0", 0), (1, "F1_1", 0), (1, "F1_2", 0), (1, "F1_3", 0),
         (1, "T1_0", 1), (1, "T1_1", 1), (2, "F1_0", 1), (2, "F1_1", 1), (3, "LT", 0), (3, "KT", 0),
         (3, "QT", 0), (3, "N", 0), (3, "V", 0), (3, "NT", 0), (4, "F1_2", 1), (4, "F1_3", 1)]
PREFIX_0 = {0: ["LT"], 2: ["KT"], 4: ["QT"], 6: ["V"], 8: ["N"], 9: ["NT"]}
SUFFIX_LAST = {1: ["WO_0"], 2: ["WO_1"], 3: ["WO_2"], 4: ["WO_3"], 6: ["T3_0"], 7: ["T3_1"],
               8: ["F2_0"], 9: ["F2_1"], 10: ["F2_2"], 12: ["F2_3"]}
LAST = [(0, name, B - 1) for name in ("WO_0", "WO_1", "WO_2", "WO_3")] + \
       [(1, name, B - 1) for name in ("T3_0", "T3_1", "F2_0", "F2_1", "F2_2", "F2_3")]

PROLOGUE, EPILOGUE = -1, B


def static(v):
    return isinstance(v, int)


def ring_base(it):
    if static(it) and it <= 0:
        return 0 if it == PROLOGUE else len(FIRST)
    if static(it) and it == EPILOGUE:
        return ring_base(B - 1) + NSUF
    return it * (NPRE + NSUF) + (NPRE - NSUF)


def jobs_of(it):
    if static(it) and it in (PROLOGUE, EPILOGUE):
        return FIRST if it == PROLOGUE else LAST
    pre, suf = PREFIX, SUFFIX
    if static(it) and it == 0:
        pre, suf = PREFIX_0, {}
    if static(it) and it == B - 1:
        pre, suf = {}, SUFFIX_LAST
    return [job for s in range(QUADS)
            for job in [(s, name, it - 1) for name in suf.get(s, [])] + [(s, name, it + 1) for name in pre.get(s, [])]]


def evac_count(name, b, it):
    if static(b) and (name, b) in [job[1:] for job in FIRST]:
        it = PROLOGUE
    jobs = [job[1:] if static(it) else job[1] for job in jobs_of(it)]
    return ring_base(it) + jobs.index((name, b) if static(it) else name) + 1


def quad_units(s):
    g, par, kt = s // 8, (s % 8) // 4, s % 4
    return g, par, kt, [8 * g + 2 * j + par for j in range(4)]


def build_macaron(nc, x, wq_t, wk_t, wv_t, wo_rows, bo, w_re, w_im, bias, cos_tab, sin_tab, ident_in,
                  head_ones_in, out):
    x_v = x.rearrange("b (p t) e -> b p (t e)", t=T)
    out_v = out.rearrange("b (p t) e -> b p (t e)", t=T)

    q_scr = nc.dram_tensor("q_scr", [HD, PARTS, S], BF16, kind="Internal").ap()
    k_scr = nc.dram_tensor("k_scr", [HD, PARTS, PARTS, S], BF16, kind="Internal").ap()

    ctx = ExitStack()
    with ctx:
        def sb(name, shape, dt=F32):
            return ctx.enter_context(nc.sbuf_tensor(name, shape, dt))

        def sem(name):
            return ctx.enter_context(nc.semaphore(name))

        ident = sb("ident", [P, P])
        head_ones = sb("head_ones", [P, 32], BF16)
        cos_sb = sb("cos_sb", [P, C, E])
        sin_sb = sb("sin_sb", [P, C, E])
        nsin_sb = sb("nsin_sb", [P, C, E])
        wre_sb = sb("wre_sb", [P, C, E])
        wim_sb = sb("wim_sb", [P, C, E])
        are_t = sb("are_t", [P, C, E])
        aim_t = sb("aim_t", [P, C, E])
        half_ffn = sb("half_ffn", [P, C, E])
        wq_sb = sb("wq_sb", [P, HD])
        wk_sb = sb("wk_sb", [P, HD])
        wv_sb = sb("wv_sb", [P, HD])
        wo_sb = sb("wo_sb", [P, E])
        bo_sb = sb("bo_sb", [P, E])
        bias_raw = sb("bias_raw", [P, E])
        waking = sb("waking", [P, S], BF16)
        half_bias = sb("half_bias", [P, E])
        power = sb("power", [P, T])
        x_in = [sb(f"x_in{i}", [P, T, E]) for i in range(2)]
        x1 = [sb(f"x1_{i}", [P, T, E]) for i in range(2)]
        x2 = sb("x2", [P, T, E])
        x_out = sb("x_out", [P, T, E])
        xh = sb("xh", [P, T, E])
        lh = sb("lh", [P, T, HD])
        stats = [sb(f"stats{i}", [P, T, 6]) for i in range(3)]
        mv = [sb(f"mv{i}", [P, T, 2]) for i in range(3)]
        veps = [sb(f"veps{i}", [P, T]) for i in range(3)]
        rstd = [sb(f"rstd{i}", [P, T]) for i in range(3)]
        xT = sb("xT", [P, T, C, P])
        leftT = sb("leftT", [P, S])
        qp = sb("qp", [P, PARTS, S], BF16)
        kp = sb("kp", [P, PARTS, S], BF16)
        rest = sb("rest", [P, S])
        sq_q = sb("sq_q", [P, S], BF16)
        sq_k = sb("sq_k", [P, S], BF16)
        QS = [sb(f"QS{i}", [P, H, S], BF16) for i in range(2)]
        KS = [sb(f"KS{i}", [P, H, S], BF16) for i in range(2)]
        VS = [sb(f"VS{i}", [P, T, H, COL]) for i in range(2)]
        probs = [sb(f"probs{i}", [P, 2, S]) for i in range(PRING)]
        ot_t = sb("ot_t", [P, S // 32, 32])
        recip = sb("recip", [P, S // 32, 2])
        on = sb("on", [P, S // 32, 32])
        otn = sb("otn", [P, S])
        norms = sb("norms", [64, 1])
        norm_row = sb("norm_row", [1, 64])
        norm_prod = sb("norm_prod", [1, H])
        worst = sb("worst", [1, 1])
        safe = sb("safe", [1, 1], I32)
        neg_max = sb("neg_max", [P, T, H])
        shift = sb("shift", [H, PARTS, S], BF16)
        shift_rest = sb("shift_rest", [H, S])
        ones_row = sb("ones_row", [H, S], BF16)

        scores = [ctx.enter_context(nc.psum_tensor(f"scores{i}", [P, 2, S], F32)) for i in range(2)]
        ot = [ctx.enter_context(nc.psum_tensor(f"ot{i}", [P, S], F32)) for i in range(2)]
        misc = [ctx.enter_context(nc.psum_tensor(f"misc{i}", [P, S], F32)) for i in range(2)]

        re_loaded = sem("re_loaded")
        im_loaded = sem("im_loaded")
        ident_loaded = sem("ident_loaded")
        small_loaded = sem("small_loaded")
        x_loaded = [sem(f"x_loaded{i}") for i in range(2)]
        ones_set = sem("ones_set")
        ks_ones = sem("ks_ones")
        consts_set = sem("consts_set")
        bias_set = sem("bias_set")
        nsin_set = sem("nsin_set")
        ffn_mm = sem("ffn_mm")
        ffn_copied = sem("ffn_copied")
        misc_ready = sem("misc_ready")
        evacuated = sem("evacuated")
        stats_done = [sem(f"stats_done{i}") for i in range(3)]
        mv_done = [sem(f"mv_done{i}") for i in range(3)]
        veps_done = [sem(f"veps_done{i}") for i in range(3)]
        rstd_done = [sem(f"rstd_done{i}") for i in range(3)]
        normed = [sem(f"normed{i}") for i in range(3)]
        xb_done = sem("xb_done")
        x2b_done = sem("x2b_done")
        qp_step = sem("qp_step")
        kp_step = sem("kp_step")
        sq_done = sem("sq_done")
        x2_begun = sem("x2_begun")
        q_stored = [sem(f"q_stored{g}") for g in range(2)]
        k_stored = [sem(f"k_stored{g}") for g in range(2)]
        rows_loaded = [sem(f"rows_loaded{g}") for g in range(2)]
        guard_step = sem("guard_step")
        shift_zeroed = sem("shift_zeroed")
        waking_set = sem("waking_set")
        max_ready = sem("max_ready")
        max_used = sem("max_used")
        maxT_ready = sem("maxT_ready")
        shift_step = sem("shift_step")
        shift_ready = sem("shift_ready")
        shift_loaded = sem("shift_loaded")
        scores_ready = sem("scores_ready")
        exp_done = sem("exp_done")
        quad_done = sem("quad_done")
        ot_taken = sem("ot_taken")
        ot_step = sem("ot_step")
        otn_ready = sem("otn_ready")
        out_stored = sem("out_stored")

        block = ctx.enter_context(nc.Block())

        def wait(eng, s, value):
            if static(value) and value <= 0:
                return
            eng.wait_ge(s, value)

        def wait_alone(eng, s, value):
            if not static(value):
                value = eng.to_reg(value)
                eng.wait_ge(ones_set, 1)
            wait(eng, s, value)

        def iterations(eng, body):
            body(0, 0)
            with eng.Fori(1, B - 1, 2) as i:
                body(i, 1)
                body(i + 1, 0)
            body(B - 1, 1)

        def bank_of(n, base):
            return misc[(n + (base if static(base) else 0)) % 2]

        def is_first(it):
            return static(it) and it == 0

        def is_last(it):
            return static(it) and it == B - 1

        @block.sync
        def _(sp):
            def load_x(b, par):
                sp.dma_start(x_in[par][:, :, :].rearrange("p t e -> p (t e)"), x_v[b]).then_inc(x_loaded[par], 16)

            def stack_parts(b, par, it):
                halves = [(g, slice(64 * g, 64 * (g + 1)), slice(8 * g, 8 * (g + 1))) for g in range(2)]
                for g, half, heads in halves:
                    wait_alone(sp, kp_step, 3 * (b + 1))
                    wait_alone(sp, rows_loaded[g], 64 * b)
                    sp.dma_start(k_scr[half].rearrange("r i j s -> r i (j s)"),
                                 kp[half, :, :].rearrange("r j s -> r (j s)").unsqueeze(1)
                                 .to_broadcast([64, PARTS, PARTS * S])).then_inc(k_stored[g], 16)
                    wait_alone(sp, qp_step, 3 * (b + 1))
                    sp.dma_start(q_scr[half], qp[half, :, :]).then_inc(q_stored[g], 16)
                    wait_alone(sp, quad_done, QUADS * (b - 1))
                    wait_alone(sp, k_stored[g], 16 * (b + 1))
                    sp.dma_start(KS[par][0:SROW, heads, :],
                                 k_scr[half].rearrange("(h d) i j s -> (d i j) h s", d=Dh)).then_inc(rows_loaded[g], 16)
                    wait_alone(sp, q_stored[g], 16 * (b + 1))
                    for j in range(PARTS):
                        sp.dma_start(QS[par][j:SROW:PARTS, heads, :],
                                     q_scr[half].rearrange("(h d) i s -> (d i) h s", d=Dh)).then_inc(rows_loaded[g], 16)

            def shift_rows(b, par):
                wait_alone(sp, shift_ready, b + 1)
                for j in range(PARTS):
                    sp.dma_start(QS[par][SROW + j:SROW + j + 1, :, :], shift[:, j, :]).then_inc(shift_loaded, 16)

            def store_out(b, it):
                for i in range(2):
                    wait_alone(sp, evacuated, evac_count(f"F2_{2 * i + 1}", b, it))
                    sp.dma_start(out_v[b][:, 2 * i * E:2 * (i + 1) * E],
                                 x_out[:, 2 * i:2 * i + 2, :].rearrange("p t e -> p (t e)")).then_inc(out_stored, 16)

            def store_last_out(b):
                for t in range(T):
                    sp.wait_ge(evacuated, evac_count(f"F2_{t}", b, EPILOGUE))
                    sp.dma_start(out_v[b][:, t * E:(t + 1) * E], x_out[:, t, :]).then_inc(out_stored, 16)

            sp.sem_inc(out_stored, 32)
            sp.dma_start(wre_sb[:, :, :], w_re.rearrange("(c p) e -> p c e", p=P)).then_inc(re_loaded, 16)
            sp.dma_start(wim_sb[:, :, :], w_im.rearrange("(c p) e -> p c e", p=P)).then_inc(im_loaded, 16)
            load_x(0, 0)
            sp.dma_start(bias_raw[:, :], bias.partition_broadcast(P)).then_inc(small_loaded, 16)
            sp.dma_start(bo_sb[:, :], bo.partition_broadcast(P)).then_inc(small_loaded, 16)
            sp.dma_start(wo_sb[:, :], wo_rows).then_inc(small_loaded, 16)
            load_x(1, 1)
            sp.wait_ge(ones_set, 1)
            for i in range(2):
                for j in range(PARTS):
                    sp.dma_start(KS[i][SROW + j:SROW + j + 1, :, :], ones_row[:, :]).then_inc(ks_ones, 16)
            stack_parts(0, 0, PROLOGUE)

            def body(it, par):
                if not (static(it) and it + 2 >= B):
                    wait_alone(sp, evacuated, ring_base(it))
                    load_x(it + 2, par)
                if not is_last(it):
                    stack_parts(it + 1, 1 - par, it)
                    shift_rows(it + 1, 1 - par)
                if not is_first(it):
                    store_out(it - 1, it)

            body(0, 0)
            with sp.Fori(1, B - 3, 2) as i:
                body(i, 1)
                body(i + 1, 0)
            for it in range(B - 3, B):
                body(it, it % 2)
            store_last_out(B - 1)
            sp.wait_ge(out_stored, 32 * B + 16 * T)

        @block.gpsimd
        def _(pool):
            nc.gpsimd.memset(ones_row[:, :], 1.0).then_inc(ones_set, 1)
            nc.gpsimd.memset(power[:, :], NORM_POWER).then_inc(consts_set, 1)
            for i in range(2):
                nc.gpsimd.memset(VS[i][:, :, :, :], 0.0).then_inc(consts_set, 1)
            pool.wait_ge(consts_set, 3)
            for i in range(2):
                for par in range(2):
                    nc.gpsimd.memset(VS[i][:, :, par::2, DEN + Dh * par:DEN + Dh * (par + 1)], 1.0).then_inc(consts_set, 1)


            def rstd_of(k, count, tiles=slice(0, T)):
                wait_alone(pool, mv_done[k], count)
                nc.gpsimd.tensor_scalar(veps[k][:, tiles], mv[k][:, tiles, 1], EPS, None, ALU.add).then_inc(veps_done[k], 1)
                wait(pool, veps_done[k], count)
                nc.gpsimd.tensor_tensor(rstd[k][:, tiles], veps[k][:, tiles], power[:, tiles], ALU.pow).then_inc(rstd_done[k], 1)

            def add_bias(buf, done, k, count, tiles=slice(0, T)):
                wait(pool, normed[k], count)
                nc.gpsimd.tensor_tensor(buf[:, tiles, :], buf[:, tiles, :],
                                        half_bias[:, :].unsqueeze(1).to_broadcast([P, tiles.stop - tiles.start, E]),
                                        ALU.add).then_inc(done, 1)

            def square(parts, sq, step, b):
                wait(pool, step, 3 * b + 1)
                nc.gpsimd.tensor_tensor(sq[:, :], parts[:, 0, :], parts[:, 0, :], ALU.mult).then_inc(sq_done, 1)

            rstd_of(0, 1)
            pool.wait_ge(small_loaded, 16 * 7)
            nc.gpsimd.tensor_scalar(half_bias[:, :], bias_raw[:, :], 0.5, None, ALU.mult).then_inc(bias_set, 1)
            pool.wait_ge(bias_set, 1)
            add_bias(x_in[0], xb_done, 0, 1)
            rstd_of(0, 2)
            add_bias(x_in[1], xb_done, 0, 2)
            rstd_of(1, 1)
            square(kp, sq_k, kp_step, 0)
            square(qp, sq_q, qp_step, 0)
            rstd_of(1, 2)

            def body(it, par, tail=True):
                if not is_first(it) and not is_last(it):
                    rstd_of(1, it + 2)
                if not is_last(it):
                    square(kp, sq_k, kp_step, it + 1)
                if not is_first(it):
                    rstd_of(2, it)
                if not is_last(it):
                    square(qp, sq_q, qp_step, it + 1)
                if not is_first(it):
                    add_bias(x2, x2b_done, 2, it)
                if tail:
                    rstd_of(0, it + 3)
                    add_bias(x_in[par], xb_done, 0, it + 3)

            body(0, 0)
            with pool.Fori(1, B - 3, 2) as i:
                body(i, 1)
                body(i + 1, 0)
            for it in range(B - 3, B):
                body(it, it % 2, tail=it + 2 < B)
            for i in range(2):
                rstd_of(2, B + i, slice(2 * i, 2 * i + 2))
            for i in range(2):
                add_bias(x2, x2b_done, 2, B + i, slice(2 * i, 2 * i + 2))

        @block.scalar
        def _(act):
            act.dma_start(cos_sb[:, :, :], cos_tab.rearrange("(c p) e -> p c e", p=P)).then_inc(re_loaded, 16)
            act.dma_start(sin_sb[:, :, :], sin_tab.rearrange("(c p) e -> p c e", p=P)).then_inc(im_loaded, 16)
            act.dma_start(ident[:, :], ident_in).then_inc(ident_loaded, 16)
            act.dma_start(head_ones[:, :], head_ones_in).then_inc(small_loaded, 16)
            act.dma_start(wq_sb[:, :], wq_t).then_inc(small_loaded, 16)
            act.dma_start(wk_sb[:, :], wk_t).then_inc(small_loaded, 16)
            act.dma_start(wv_sb[:, :], wv_t).then_inc(small_loaded, 16)
            act.wait_ge(im_loaded, 32)
            nc.scalar.mul(nsin_sb[:, :, :], sin_sb[:, :, :], -1.0).then_inc(nsin_set, 1)
            act.wait_ge(ffn_mm, 1)
            nc.scalar.copy(are_t[:, :, :], scores[0][:, :, 0:E]).then_inc(ffn_copied, 1)
            act.wait_ge(ffn_mm, 2)
            nc.scalar.copy(aim_t[:, :, :], scores[1][:, :, 0:E]).then_inc(ffn_copied, 1)
            act.wait_ge(ffn_mm, 3)
            nc.scalar.mul(half_ffn[:, :, :], scores[0][:, :, 0:E],
                          0.5 / E).then_inc(ffn_copied, 1)

            act.wait_ge(shift_ready, 1)
            for j in range(PARTS):
                act.dma_start(QS[0][SROW + j:SROW + j + 1, :, :], shift[:, j, :]).then_inc(shift_loaded, 16)

            def body(b, par):
                for u in range(PAIRS):
                    wait(act, scores_ready, PAIRS * b + u + 1)
                    wait(act, quad_done, QUADS * b + (u - PRING) // 2 + 1)
                    nc.scalar.activation(probs[u % PRING][:, :, :], scores[u % 2][:, :, :], ACT.Exp,
                                         scale=SCORE_SCALE).then_inc(exp_done, 1)

            iterations(act, body)

        @block.tensor
        def _(pe):
            mm = nc.tensor.matmul

            def spectral(o, k, lhsT, rhs):
                for m in range(C):
                    for c in range(C):
                        last = mm(o[:, m, 0:E], lhsT[:, c, m * P:(m + 1) * P], rhs[:, c, :],
                                  start=(k, c) == (0, 0), stop=(k, c) == (1, C - 1))
                return last

            def keep_awake(n, bank=ot[1][:, :]):
                for _ in range(n):
                    mm(bank, waking[:, 0:P], waking[:, :], start=True, stop=True)

            pe.wait_ge(waking_set, 1)
            keep_awake(8)
            pe.wait_ge(re_loaded, 32)
            spectral(scores[0], 0, wre_sb, cos_sb)
            pe.wait_ge(im_loaded, 32)
            spectral(scores[0], 1, wim_sb, sin_sb).then_inc(ffn_mm, 1)
            spectral(scores[1], 0, wim_sb, cos_sb)
            pe.wait_ge(nsin_set, 1)
            spectral(scores[1], 1, wre_sb, nsin_sb).then_inc(ffn_mm, 1)

            def job(name, n, base, b, it):
                bank = bank_of(n, base)

                def after(done):
                    (wait_alone if name == "NT" else wait)(pe, evacuated, evac_count(done, b, it))

                (wait_alone if name in ("N", "NT") else wait)(pe, evacuated, base + n - 1)
                kind, i = name[:2], int(name[-1]) if "_" in name else 0
                if kind in ("T1", "T3"):
                    wait(pe, normed[0 if kind == "T1" else 2], b + 1 + (i if static(it) and it == EPILOGUE else 0))
                    for t in range(2):
                        for c in range(C):
                            last = nc.tensor.transpose(bank[:, (C * t + c) * P:(C * t + c + 1) * P],
                                                       xh[:, 2 * i + t, c * P:(c + 1) * P], ident[:, :])
                elif kind in ("F1", "F2"):
                    after(("T1" if kind == "F1" else "T3") + f"_{i // 2}")
                    for c in range(C):
                        last = mm(bank[:, 0:E], xT[:, i, c, :], half_ffn[:, c, :], start=c == 0, stop=c == C - 1)
                elif kind == "WO":
                    wait(pe, otn_ready, b + 1)
                    last = mm(bank[:, 0:E], otn[:, i * P:(i + 1) * P], wo_sb[:, :], start=True, stop=True)
                elif name == "LT":
                    wait(pe, normed[1], b + 1)
                    for t in range(T):
                        last = nc.tensor.transpose(bank[:, t * P:(t + 1) * P], lh[:, t, :], ident[:, :])
                elif name in ("QT", "KT"):
                    after("LT")
                    last = mm(bank[:, :], (wq_sb if name == "QT" else wk_sb)[:, :], leftT[:, :], start=True, stop=True)
                elif name == "V":
                    for t in range(T):
                        last = mm(bank[:, t * HD:(t + 1) * HD], leftT[:, t * P:(t + 1) * P], wv_sb[:, :],
                                  start=True, stop=True)
                elif name == "N":
                    wait_alone(pe, sq_done, 2 * (b + 1))
                    mm(bank[0:32, :], head_ones[:, :], sq_q[:, :], start=True, stop=True)
                    last = mm(bank[32:64, :], head_ones[:, :], sq_k[:, :], start=True, stop=True)
                elif name == "NT":
                    after("N")
                    last = mm(bank[0:1, 0:64], norms[:, :], ident[0:64, 0:64], start=True, stop=True)
                last.then_inc(misc_ready, 1)

            def score_pair(b, par, u):
                g, _, kt, heads = quad_units(u // 2)
                if u in (0, PAIRS // 2):
                    rows_ready(b, g)
                wait(pe, exp_done, PAIRS * b + u - 1)
                for i in range(2):
                    h = heads[2 * (u % 2) + i]
                    last = mm(scores[u % 2][:, i, :], KS[par][0:ROWS, h, kt * P:(kt + 1) * P],
                              QS[par][0:ROWS, h, :], start=True, stop=True)
                last.then_inc(scores_ready, 1)

            def rows_ready(b, g):
                wait(pe, rows_loaded[g], 64 * (b + 1))
                if g == 0:
                    wait(pe, shift_loaded, 48 * (b + 1))

            def value_quad(b, par, s):
                g, p, kt, heads = quad_units(s)
                if s == 0:
                    wait(pe, evacuated, evac_count("V", 0, PROLOGUE) if is_first(b) else ring_base(b))
                if s % 8 == 0:
                    wait(pe, ot_taken, 2 * b + g - 1)
                wait(pe, exp_done, PAIRS * b + 2 * s + 2)
                for j, h in enumerate(heads):
                    last = mm(ot[g][COL * j:COL * (j + 1), :], VS[par][:, kt, h, :],
                              probs[(2 * s + j // 2) % PRING][:, j % 2, :], start=s % 8 == 0, stop=s % 8 == 7)
                last.then_inc(quad_done, 1)

            def maxima(b, par, base):
                wait_alone(pe, guard_step, 3 * (b + 1))
                small = pe.value_load(safe[0:1, 0:1], min_val=0, max_val=1)
                with pe.If(small == 0):
                    wait(pe, evacuated, base)
                    wait(pe, rows_loaded[0], 64 * (b + 1))
                    wait(pe, rows_loaded[1], 64 * (b + 1))
                    for h in range(H):
                        for t in range(T):
                            n = h * T + t
                            if n >= 2:
                                wait(pe, max_used, H * T * b + n - 1)
                            mm(misc[n % 2][:, :], QS[par][0:SROW, h, t * P:(t + 1) * P], KS[par][0:SROW, h, :],
                               start=True, stop=True).then_inc(max_ready, 1)
                    wait(pe, max_used, H * T * (b + 1))
                    for t in range(T):
                        last = mm(misc[0][0:H, t * P:(t + 1) * P], neg_max[:, t, :], ident[:, :], start=True, stop=True)
                    last.then_inc(maxT_ready, 1)
                    wait(pe, shift_step, 3 * b + 2)
                with pe.Else():
                    pe.sem_inc(max_ready, H * T)
                    pe.sem_inc(maxT_ready, 1)

            def run_jobs(it, s, between={}):
                for n, (at, name, b) in enumerate(jobs_of(it)):
                    if at == s:
                        keep_awake(between.get(name, 0))
                        job(name, n, ring_base(it), b, it)

            pe.wait_ge(ident_loaded, 16)
            run_jobs(PROLOGUE, 0)
            pe.wait_ge(ffn_copied, 2)
            spectral(scores[0], 0, are_t, cos_sb)
            spectral(scores[0], 1, aim_t, nsin_sb).then_inc(ffn_mm, 1)
            pe.wait_ge(ffn_copied, 3)
            pe.wait_ge(small_loaded, 16 * 7)
            pe.wait_ge(consts_set, 7)
            run_jobs(PROLOGUE, 1)
            run_jobs(PROLOGUE, 2)
            run_jobs(PROLOGUE, 3, between={"N": 7})
            keep_awake(8)
            maxima(0, 0, evac_count("NT", 0, PROLOGUE))
            run_jobs(PROLOGUE, 4)
            keep_awake(12)
            pe.wait_ge(ks_ones, 96)
            score_pair(0, 0, 0)
            score_pair(0, 0, 1)

            def body(it, par):
                for s in range(QUADS):
                    for u in (2 * s + 2, 2 * s + 3):
                        if u < PAIRS:
                            score_pair(it, par, u)
                    if s == QUADS - 1 and not is_last(it):
                        score_pair(it + 1, 1 - par, 0)
                        score_pair(it + 1, 1 - par, 1)
                    value_quad(it, par, s)
                    if s == GUARD_SLOT + 1 and not is_last(it):
                        maxima(it + 1, 1 - par, ring_base(it) + len([1 for job in jobs_of(it) if job[0] <= GUARD_SLOT]))
                    run_jobs(it, s)

            iterations(pe, body)
            keep_awake(8, scores[0][:, 0, :])
            run_jobs(EPILOGUE, 0)
            keep_awake(12, scores[0][:, 0, :])
            run_jobs(EPILOGUE, 1)

        @block.vector
        def _(dve):
            def got(n, base):
                wait(dve, misc_ready, base + n + 1)

            def norm_stats(k, src, t, last):
                ins = nc.vector.bn_stats(stats[k][:, t, :], src[:, t, :])
                if last:
                    ins.then_inc(stats_done[k], 1)

            def norm_moments(k, count, tiles=range(T)):
                wait_alone(dve, stats_done[k], count)
                for t in tiles:
                    last = nc.vector.bn_aggr(mv[k][:, t, :], stats[k][:, t, :])
                last.then_inc(mv_done[k], 1)

            def norm_apply(k, src, dst, width, count, tiles=range(T)):
                wait(dve, rstd_done[k], count)
                for t in tiles:
                    last = nc.vector.tensor_scalar(dst[:, t, 0:width], src[:, t, 0:width], mv[k][:, t, 0:1],
                                                   rstd[k][:, t:t + 1], ALU.subtract, ALU.mult)
                last.then_inc(normed[k], 1)

            def norm0(b, par):
                wait(dve, x_loaded[par], 8 * (b - par) + 16)
                for t in range(T):
                    norm_stats(0, x_in[par], t, t == T - 1)
                norm_moments(0, b + 1)
                norm_apply(0, x_in[par], xh, E, b + 1)

            def split(bank, parts, step, b, count):
                wait(dve, rows_loaded[0], 64 * b)
                wait(dve, rows_loaded[1], 64 * b)
                nc.vector.tensor_copy(parts[:, 0, :], bank[:, :]).then_inc(step, 1)
                wait(dve, step, 3 * b + 1)
                nc.vector.tensor_tensor(rest[:, :], bank[:, :], parts[:, 0, :], ALU.subtract).then_inc(evacuated, 1)
                wait(dve, evacuated, count)
                nc.vector.tensor_copy(parts[:, 1, :], rest[:, :]).then_inc(step, 1)
                wait(dve, step, 3 * b + 2)
                nc.vector.tensor_tensor(parts[:, 2, :], rest[:, :], parts[:, 1, :], ALU.subtract).then_inc(step, 1)

            def evacuate(name, n, base, b, par, it):
                bank = bank_of(n, base)
                got(n, base)
                kind, i = name[:2], int(name[-1]) if "_" in name else 0
                tile = bank[:, 0:E]
                if kind in ("T1", "T3"):
                    nc.vector.tensor_copy(xT[:, 2 * i:2 * i + 2, :, :],
                                          bank[:, :].rearrange("p (t c q) -> p t c q", t=2, c=C)).then_inc(evacuated, 1)
                elif kind == "F1":
                    wait(dve, xb_done, b + 1)
                    wait(dve, x2_begun, b - 1)
                    nc.vector.tensor_tensor(x1[par][:, i, :], tile, x_in[par][:, i, :], ALU.add).then_inc(evacuated, 1)
                elif kind == "WO":
                    wait(dve, x2_begun, b + 1)
                    nc.vector.tensor_tensor(x2[:, i, :], tile, x2[:, i, :], ALU.add).then_inc(evacuated, 1)
                elif kind == "F2":
                    wait(dve, x2b_done, b + 1 + (i // 2 if static(it) and it == EPILOGUE else 0))
                    wait(dve, out_stored, 32 * (b + 1))
                    nc.vector.tensor_tensor(x_out[:, i, :], tile, x2[:, i, :], ALU.add).then_inc(evacuated, 1)
                elif name == "LT":
                    nc.vector.tensor_copy(leftT[:, :], bank[:, :]).then_inc(evacuated, 1)
                    wait(dve, shift_loaded, 48 * b)
                    nc.vector.memset(shift[:, :, :].bitcast(I32), 0).then_inc(shift_zeroed, 1)
                elif name == "QT":
                    split(bank, qp, qp_step, b, base + n + 1)
                elif name == "KT":
                    wait(dve, sq_done, 2 * b)
                    split(bank, kp, kp_step, b, base + n + 1)
                elif name == "V":
                    if not (static(b) and b < 2):
                        wait(dve, quad_done, QUADS * (b - 1))
                    for r in range(2):
                        last = nc.vector.tensor_copy(
                            VS[par][:, :, r::2, Dh * r:Dh * (r + 1)],
                            bank[:, :].rearrange("p (t h r d) -> p t h r d", t=T, r=2, d=Dh)[:, :, :, r, :])
                    last.then_inc(evacuated, 1)
                elif name == "N":
                    nc.vector.reduce_max(norms[:, :], bank[0:64, :], AX.X).then_inc(evacuated, 1)
                elif name == "NT":
                    nc.vector.tensor_copy(norm_row[:, :], bank[0:1, 0:64]).then_inc(evacuated, 1)
                    wait(dve, evacuated, base + n + 1)
                    nc.vector.tensor_tensor(norm_prod[:, :], norm_row[:, 0:H], norm_row[:, 32:32 + H], ALU.mult).then_inc(guard_step, 1)
                    wait(dve, guard_step, 3 * b + 1)
                    nc.vector.reduce_max(worst[:, :], norm_prod[:, :], AX.X).then_inc(guard_step, 1)
                    wait(dve, guard_step, 3 * b + 2)
                    nc.vector.tensor_scalar(safe[:, :], worst[:, :], SAFE_PRODUCT, None, ALU.is_le).then_inc(guard_step, 1)

            def normalize(b, g):
                wait(dve, quad_done, QUADS * b + 8 * (g + 1))
                nc.vector.transpose(ot_t[:, :, :].rearrange("p c r -> p (c r)"), ot[g][:, :]).then_inc(ot_taken, 1)
                wait(dve, ot_taken, 2 * b + g + 1)
                nc.vector.reciprocal(recip[:, :, :], ot_t[:, :, DEN::Dh]).then_inc(ot_step, 1)
                wait(dve, ot_step, 4 * b + 2 * g + 1)
                wait(dve, otn_ready, b)
                nc.vector.tensor_tensor(on[:, :, DEN * g:DEN * (g + 1)].rearrange("p c (r d) -> p c r d", d=Dh),
                                        ot_t[:, :, 0:DEN].rearrange("p c (r d) -> p c r d", d=Dh),
                                        recip[:, :, :].unsqueeze(3).to_broadcast([P, S // 32, 2, Dh]),
                                        ALU.mult).then_inc(ot_step, 1)
                if g == 1:
                    wait(dve, ot_step, 4 * b + 4)
                    nc.vector.transpose(otn[:, :], on[:, :, :].rearrange("p c r -> p (c r)")).then_inc(otn_ready, 1)

            def begin_x2(par):
                nc.vector.tensor_tensor(x2[:, :, :], x1[par][:, :, :], bo_sb[:, :].unsqueeze(1).to_broadcast([P, T, E]),
                                        ALU.add).then_inc(x2_begun, 1)

            def guard(b):
                wait_alone(dve, guard_step, 3 * (b + 1))
                wait_alone(dve, shift_zeroed, b + 1)
                small = dve.value_load(safe[0:1, 0:1], min_val=0, max_val=1)
                with dve.If(small == 0):
                    for n in range(H * T):
                        wait(dve, max_ready, H * T * b + n + 1)
                        nc.vector.tensor_reduce(neg_max[:, n % T, n // T:n // T + 1], misc[n % 2][:, :], AX.X, ALU.max,
                                                negate=True).then_inc(max_used, 1)
                    wait(dve, maxT_ready, b + 1)
                    bank = misc[0][0:H, :]
                    nc.vector.tensor_copy(shift[:, 0, :], bank).then_inc(shift_step, 1)
                    wait(dve, shift_step, 3 * b + 1)
                    nc.vector.tensor_tensor(shift_rest[:, :], bank, shift[:, 0, :], ALU.subtract).then_inc(shift_step, 1)
                    wait(dve, shift_step, 3 * b + 2)
                    nc.vector.tensor_copy(shift[:, 1, :], shift_rest[:, :]).then_inc(shift_step, 1)
                    wait(dve, shift_step, 3 * b + 3)
                    nc.vector.tensor_tensor(shift[:, 2, :], shift_rest[:, :], shift[:, 1, :], ALU.subtract).then_inc(shift_ready, 1)
                with dve.Else():
                    dve.sem_inc(shift_step, 3)
                    dve.sem_inc(max_used, H * T)
                    dve.sem_inc(shift_ready, 1)

            def run_jobs(it, par, s):
                for n, (at, name, b) in enumerate(jobs_of(it)):
                    if at != s:
                        continue
                    jpar = b % 2 if static(b) else 1 - par
                    evacuate(name, n, ring_base(it), b, jpar, it)
                    kind = name[:2]
                    if kind not in ("F1", "WO") or (static(it) and it == EPILOGUE):
                        continue
                    k, src = (1, x1[jpar]) if kind == "F1" else (2, x2)
                    i = int(name[-1])
                    for t in ([i - 1] if i else []) + ([i] if i == T - 1 else []):
                        wait(dve, evacuated, evac_count(f"{kind}_{t}", b, it))
                        norm_stats(k, src, t, t == T - 1)
                    if i == T - 1:
                        norm_moments(k, b + 1)
                        if kind == "F1" and not (static(it) and it == PROLOGUE):
                            norm_apply(1, src, lh, HD, b + 1)

            def last_suffix():
                b, jobs, base = B - 1, [job[1] for job in LAST], ring_base(EPILOGUE)

                def take(name):
                    evacuate(name, jobs.index(name), base, b, b % 2, EPILOGUE)

                for i in range(2):
                    tiles = range(2 * i, 2 * i + 2)
                    for t in tiles:
                        take(f"WO_{t}")
                    for t in tiles:
                        wait(dve, evacuated, evac_count(f"WO_{t}", b, EPILOGUE))
                        norm_stats(2, x2, t, t == tiles[-1])
                    norm_moments(2, b + 1 + i, tiles)
                for i in range(2):
                    norm_apply(2, x2, xh, E, b + 1 + i, range(2 * i, 2 * i + 2))
                for name in jobs[T:]:
                    take(name)

            nc.vector.memset(waking[:, :].bitcast(I32), 0).then_inc(waking_set, 1)
            dve.wait_ge(consts_set, 7)
            norm0(0, 0)
            run_jobs(PROLOGUE, 0, 0)
            norm0(1, 1)
            run_jobs(PROLOGUE, 0, 1)
            norm_apply(1, x1[0], lh, HD, 1)
            run_jobs(PROLOGUE, 0, 2)
            run_jobs(PROLOGUE, 0, 3)
            guard(0)
            run_jobs(PROLOGUE, 0, 4)
            norm_apply(1, x1[1], lh, HD, 2)

            def body(it, par, tail=True):
                for s in range(QUADS):
                    if s == 0 and not is_first(it):
                        normalize(it - 1, 1)
                    run_jobs(it, par, s)
                    if s == (5 if is_last(it) else 7) and not is_first(it):
                        norm_apply(2, x2, xh, E, it)
                    if s == 9:
                        normalize(it, 0)
                    if s == 0 and not is_first(it):
                        begin_x2(1 - par)
                    if s == GUARD_SLOT and not is_last(it):
                        guard(it + 1)
                    if s == NORM0_SLOT and tail:
                        norm0(it + 2, par)

            body(0, 0)
            with dve.Fori(1, B - 3, 2) as i:
                body(i, 1)
                body(i + 1, 0)
            for it in range(B - 3, B):
                body(it, it % 2, tail=it + 2 < B)
            dve.wait_ge(evacuated, ring_base(EPILOGUE))
            begin_x2((B - 1) % 2)
            normalize(B - 1, 1)
            last_suffix()


def kernel(L0_attn_x, L0_attn_Wq, L0_attn_Wk, L0_attn_Wv, L0_attn_Wo, L0_attn_bo,
           L0_ffn_w_freq_real, L0_ffn_w_freq_imag, L0_ffn_bias):
    import numpy as np
    import concourse.bacc as bacc
    from concourse.bass_utils import run_bass_kernel_spmd

    wo_rows = np.zeros((P, E), np.float32)
    wo = np.asarray(L0_attn_Wo)
    for h in range(H):
        g, j, par = h // 8, (h % 8) // 2, h % 2
        r = COL * j + DEN * g + Dh * par
        wo_rows[r:r + Dh, :] = wo[:, h * Dh:(h + 1) * Dh].T

    angle = 2.0 * np.pi * (np.outer(np.arange(E), np.arange(E)) % E) / E
    head_ones = np.zeros((P, 32), np.float32)
    head_ones[np.arange(P), np.arange(P) // Dh] = 1.0

    import ml_dtypes
    arrays = {
        "x": np.ascontiguousarray(L0_attn_x),
        "wq_t": np.ascontiguousarray(np.asarray(L0_attn_Wq).T),
        "wk_t": np.ascontiguousarray(np.asarray(L0_attn_Wk).T),
        "wv_t": np.ascontiguousarray(np.asarray(L0_attn_Wv).T),
        "wo_rows": wo_rows,
        "bo": np.ascontiguousarray(L0_attn_bo),
        "w_re": np.ascontiguousarray(L0_ffn_w_freq_real),
        "w_im": np.ascontiguousarray(L0_ffn_w_freq_imag),
        "bias": np.ascontiguousarray(L0_ffn_bias),
        "cos_tab": np.cos(angle).astype(np.float32),
        "sin_tab": np.sin(angle).astype(np.float32),
        "ident_in": np.eye(P, dtype=np.float32),
        "head_ones_in": head_ones.astype(ml_dtypes.bfloat16),
    }
    nc = bacc.Bacc("TRN2", target_bir_lowering=False, num_devices=1)
    args = [nc.dram_tensor(n, a.shape, mybir.dt.from_np(a.dtype), kind="ExternalInput").ap()
            for n, a in arrays.items()]
    out = nc.dram_tensor("out", (B, S, E), F32, kind="ExternalOutput").ap()
    build_macaron(nc, *args, out)
    r = run_bass_kernel_spmd(nc, [arrays], core_ids=[0])
    return r.results[0]["out"]
```
